# Optimizing a Trainium2 kernel written in Bass

```python
import numpy as np
import jax
import jax.numpy as jnp

def _softmax(x, axis=-1):
    return jax.nn.softmax(x, axis=axis)

def _gelu(x):
    return jax.nn.gelu(x, approximate=True)

def _silu(x):
    return jax.nn.silu(x)

def _sigmoid(x):
    return jax.nn.sigmoid(x)

def _layernorm(x, axis=-1, eps=1e-05):
    m = jnp.mean(x, axis=axis, keepdims=True)
    v = jnp.var(x, axis=axis, keepdims=True)
    return (x - m) / jnp.sqrt(v + eps)

def _scatter_add(tgt, idx, src, axis=0):
    return tgt.at[idx].add(src)

def _segment_sum(src, seg, n):
    return jax.ops.segment_sum(src, seg, n)
kernel_name = 'mk_macaron_d1_jaxref_r8_881c6b'

def setup_inputs(seed: int=0):
    np.random.seed(seed)
    _w = jnp.asarray

    def _L0_attn_setup():
        import jax, jax.numpy as jnp
        import numpy as np
        import math
        N_HEAD = 16
        N_KV_HEAD = 4
        HEAD_DIM = 64
        ROPE_THETA = 10000.0

        def _rope_cache(T, D, dtype):
            inv_freq = 1.0 / ROPE_THETA ** (jnp.arange(0, D, 2, dtype=dtype) / D)
            t = jnp.arange(T, dtype=dtype)
            freqs = jnp.einsum('i,j->ij', t, inv_freq)
            return (jnp.cos(freqs)[None, None], jnp.sin(freqs)[None, None])

        def _apply_rope(x, cos, sin):
            x1 = x[..., ::2]
            x2 = x[..., 1::2]
            return jnp.concatenate([x1 * cos - x2 * sin, x1 * sin + x2 * cos], axis=-1)
        key = jax.random.key(seed)
        k0, k1, k2, k3, k4 = jax.random.split(key, 5)
        B, T, C = (4, 256, 128)
        scale = 0.02
        return {'x': jax.random.normal(k0, (B, T, C), dtype=jnp.float32), 'Wq': jax.random.normal(k1, (C, N_HEAD * HEAD_DIM), dtype=jnp.float32) * scale, 'Wk': jax.random.normal(k2, (C, N_KV_HEAD * HEAD_DIM), dtype=jnp.float32) * scale, 'Wv': jax.random.normal(k3, (C, N_KV_HEAD * HEAD_DIM), dtype=jnp.float32) * scale, 'Wo': jax.random.normal(k4, (N_HEAD * HEAD_DIM, C), dtype=jnp.float32) * scale}
    _L0_attn_in = _L0_attn_setup()

    def _L0_ffn_setup():
        import jax, jax.numpy as jnp
        import numpy as np
        B, S, H = (2, 64, 128)
        E, I = (64, 64)
        K = 8
        G, TG = (8, 4)
        SCALE = 2.5
        T = B * S
        CAP = 64

        def _moe_forward(x, router_w, gate_w, up_w, down_w, shared_gate_w, shared_up_w, shared_down_w):
            b, s, h = x.shape
            tokens = x.reshape(-1, h)
            t = tokens.shape[0]
            logits = tokens @ router_w
            scores = jax.nn.sigmoid(logits)
            eg = E // G
            group_scores = scores.reshape(t, G, eg).max(axis=-1)
            _, sel_groups = jax.lax.top_k(group_scores, TG)
            group_mask = jnp.zeros((t, G), bool).at[jnp.arange(t)[:, None], sel_groups].set(True)
            expert_mask = jnp.repeat(group_mask, eg, axis=1)
            masked_scores = jnp.where(expert_mask, scores, 0.0)
            topk_w, topk_idx = jax.lax.top_k(masked_scores, K)
            topk_w = topk_w / jnp.clip(topk_w.sum(-1, keepdims=True), 1e-09)
            topk_w = topk_w * SCALE
            flat_e = topk_idx.reshape(-1)
            onehot = jax.nn.one_hot(flat_e, E, dtype=jnp.int32)
            prior = jnp.cumsum(onehot, axis=0) - onehot
            pos = jnp.take_along_axis(prior, flat_e[:, None], axis=1)[:, 0]
            valid = (pos < CAP).astype(tokens.dtype)
            pos_c = jnp.minimum(pos, CAP - 1)
            tidx = jnp.repeat(jnp.arange(t), K)
            dispatch = jnp.zeros((E, CAP, h), tokens.dtype)
            dispatch = dispatch.at[flat_e, pos_c].add(tokens[tidx] * valid[:, None])
            g = jnp.einsum('ech,ehi->eci', dispatch, gate_w)
            u = jnp.einsum('ech,ehi->eci', dispatch, up_w)
            expert_out = jnp.einsum('eci,eih->ech', jax.nn.silu(g) * u, down_w)
            gathered = expert_out[flat_e, pos_c]
            contrib = gathered * (topk_w.reshape(-1) * valid)[:, None]
            output = jnp.zeros((t, h), tokens.dtype).at[tidx].add(contrib)
            sg = jax.nn.silu(tokens @ shared_gate_w) * (tokens @ shared_up_w)
            output = output + sg @ shared_down_w
            return output.reshape(b, s, h)
        key = jax.random.key(seed)
        ks = jax.random.split(key, 9)
        s_h = 1.0 / np.sqrt(H)
        s_i = 1.0 / np.sqrt(I)
        return {'x': jax.random.normal(ks[0], (B, S, H), jnp.float32), 'router_w': jax.random.normal(ks[1], (H, E), jnp.float32) * s_h, 'gate_w': jax.random.normal(ks[2], (E, H, I), jnp.float32) * s_h, 'up_w': jax.random.normal(ks[3], (E, H, I), jnp.float32) * s_h, 'down_w': jax.random.normal(ks[4], (E, I, H), jnp.float32) * s_i, 'shared_gate_w': jax.random.normal(ks[5], (H, I), jnp.float32) * s_h, 'shared_up_w': jax.random.normal(ks[6], (H, I), jnp.float32) * s_h, 'shared_down_w': jax.random.normal(ks[7], (I, H), jnp.float32) * s_i}
    _L0_ffn_in = _L0_ffn_setup()
    _d = {'L0_attn_x': _L0_attn_in['x'], 'L0_attn_Wq': _L0_attn_in['Wq'], 'L0_attn_Wk': _L0_attn_in['Wk'], 'L0_attn_Wv': _L0_attn_in['Wv'], 'L0_attn_Wo': _L0_attn_in['Wo'], 'L0_ffn_router_w': _L0_ffn_in['router_w'], 'L0_ffn_gate_w': _L0_ffn_in['gate_w'], 'L0_ffn_up_w': _L0_ffn_in['up_w'], 'L0_ffn_down_w': _L0_ffn_in['down_w'], 'L0_ffn_shared_gate_w': _L0_ffn_in['shared_gate_w'], 'L0_ffn_shared_up_w': _L0_ffn_in['shared_up_w'], 'L0_ffn_shared_down_w': _L0_ffn_in['shared_down_w']}
    _x0 = _d['L0_attn_x']
    _d['L0_attn_x'] = jax.random.normal(jax.random.fold_in(jax.random.key(seed), 1), (8, 256, 128), dtype=_x0.dtype)
    del _x0
    return _d

def reference(L0_attn_x, L0_attn_Wq, L0_attn_Wk, L0_attn_Wv, L0_attn_Wo, L0_ffn_router_w, L0_ffn_gate_w, L0_ffn_up_w, L0_ffn_down_w, L0_ffn_shared_gate_w, L0_ffn_shared_up_w, L0_ffn_shared_down_w):

    def _L0_attn_ref(x, Wq, Wk, Wv, Wo):
        import jax, jax.numpy as jnp
        import numpy as np
        import math
        N_HEAD = 16
        N_KV_HEAD = 4
        HEAD_DIM = 64
        ROPE_THETA = 10000.0

        def _rope_cache(T, D, dtype):
            inv_freq = 1.0 / ROPE_THETA ** (jnp.arange(0, D, 2, dtype=dtype) / D)
            t = jnp.arange(T, dtype=dtype)
            freqs = jnp.einsum('i,j->ij', t, inv_freq)
            return (jnp.cos(freqs)[None, None], jnp.sin(freqs)[None, None])

        def _apply_rope(x, cos, sin):
            x1 = x[..., ::2]
            x2 = x[..., 1::2]
            return jnp.concatenate([x1 * cos - x2 * sin, x1 * sin + x2 * cos], axis=-1)
        B, T, C = x.shape
        H, Hkv, D = (N_HEAD, N_KV_HEAD, HEAD_DIM)
        q = (x @ Wq).reshape(B, T, H, D).transpose(0, 2, 1, 3)
        k = (x @ Wk).reshape(B, T, Hkv, D).transpose(0, 2, 1, 3)
        v = (x @ Wv).reshape(B, T, Hkv, D).transpose(0, 2, 1, 3)
        rep = H // Hkv
        k = jnp.repeat(k, rep, axis=1)
        v = jnp.repeat(v, rep, axis=1)
        cos, sin = _rope_cache(T, D, x.dtype)
        q = _apply_rope(q, cos, sin)
        k = _apply_rope(k, cos, sin)
        att = jnp.einsum('bhtd,bhsd->bhts', q, k) / math.sqrt(D)
        mask = jnp.tril(jnp.ones((T, T), dtype=bool))
        att = jnp.where(mask, att, -jnp.inf)
        att = jax.nn.softmax(att, axis=-1)
        y = jnp.einsum('bhts,bhsd->bhtd', att, v)
        y = y.transpose(0, 2, 1, 3).reshape(B, T, H * D)
        return y @ Wo

    def _L0_ffn_ref(x, router_w, gate_w, up_w, down_w, shared_gate_w, shared_up_w, shared_down_w):
        import jax, jax.numpy as jnp
        import numpy as np
        B, S, H = (2, 64, 128)
        E, I = (64, 64)
        K = 8
        G, TG = (8, 4)
        SCALE = 2.5
        T = B * S
        CAP = 64

        def _moe_forward(x, router_w, gate_w, up_w, down_w, shared_gate_w, shared_up_w, shared_down_w):
            b, s, h = x.shape
            tokens = x.reshape(-1, h)
            t = tokens.shape[0]
            logits = tokens @ router_w
            scores = jax.nn.sigmoid(logits)
            eg = E // G
            group_scores = scores.reshape(t, G, eg).max(axis=-1)
            _, sel_groups = jax.lax.top_k(group_scores, TG)
            group_mask = jnp.zeros((t, G), bool).at[jnp.arange(t)[:, None], sel_groups].set(True)
            expert_mask = jnp.repeat(group_mask, eg, axis=1)
            masked_scores = jnp.where(expert_mask, scores, 0.0)
            topk_w, topk_idx = jax.lax.top_k(masked_scores, K)
            topk_w = topk_w / jnp.clip(topk_w.sum(-1, keepdims=True), 1e-09)
            topk_w = topk_w * SCALE
            flat_e = topk_idx.reshape(-1)
            onehot = jax.nn.one_hot(flat_e, E, dtype=jnp.int32)
            prior = jnp.cumsum(onehot, axis=0) - onehot
            pos = jnp.take_along_axis(prior, flat_e[:, None], axis=1)[:, 0]
            valid = (pos < CAP).astype(tokens.dtype)
            pos_c = jnp.minimum(pos, CAP - 1)
            tidx = jnp.repeat(jnp.arange(t), K)
            dispatch = jnp.zeros((E, CAP, h), tokens.dtype)
            dispatch = dispatch.at[flat_e, pos_c].add(tokens[tidx] * valid[:, None])
            g = jnp.einsum('ech,ehi->eci', dispatch, gate_w)
            u = jnp.einsum('ech,ehi->eci', dispatch, up_w)
            expert_out = jnp.einsum('eci,eih->ech', jax.nn.silu(g) * u, down_w)
            gathered = expert_out[flat_e, pos_c]
            contrib = gathered * (topk_w.reshape(-1) * valid)[:, None]
            output = jnp.zeros((t, h), tokens.dtype).at[tidx].add(contrib)
            sg = jax.nn.silu(tokens @ shared_gate_w) * (tokens @ shared_up_w)
            output = output + sg @ shared_down_w
            return output.reshape(b, s, h)
        return _moe_forward(x, router_w, gate_w, up_w, down_w, shared_gate_w, shared_up_w, shared_down_w)
    x = L0_attn_x
    x = x + 0.5 * _L0_ffn_ref(_layernorm(x, axis=-1), L0_ffn_router_w, L0_ffn_gate_w, L0_ffn_up_w, L0_ffn_down_w, L0_ffn_shared_gate_w, L0_ffn_shared_up_w, L0_ffn_shared_down_w)
    x = x + _L0_attn_ref(_layernorm(x, axis=-1), L0_attn_Wq, L0_attn_Wk, L0_attn_Wv, L0_attn_Wo)
    x = x + 0.5 * _L0_ffn_ref(_layernorm(x, axis=-1), L0_ffn_router_w, L0_ffn_gate_w, L0_ffn_up_w, L0_ffn_down_w, L0_ffn_shared_gate_w, L0_ffn_shared_up_w, L0_ffn_shared_down_w)
    return x

_drawn_inputs = setup_inputs


def setup_inputs(seed=0):
    import zlib

    import numpy as np

    out = dict(_drawn_inputs(seed))
    spreads = {}
    factors = {'L0_attn_Wq': 8.0, 'L0_attn_Wk': 8.0}
    for name, (base, spread) in spreads.items():
        noise = np.random.default_rng([zlib.crc32(name.encode()), seed]).standard_normal(out[name].shape)
        drawn = base * np.exp(spread * noise) if base else spread * noise
        out[name] = jnp.asarray(drawn.astype(out[name].dtype))
    for name, factor in factors.items():
        out[name] = (out[name] * factor).astype(out[name].dtype)
    return out
```

```python
import concourse.bass as bass
from concourse import mybir
from contextlib import ExitStack


def macaron_block(nc, x_in, wq_in, wkv_in, wo_in, router_in, gu_in, down_in, sg_in, su_in, sd_in, const_in, out):
    f32 = mybir.dt.float32
    bf16 = mybir.dt.bfloat16
    u32 = mybir.dt.uint32
    i32 = mybir.dt.int32
    ALU = mybir.AluOpType
    ACT = mybir.ActivationFunctionType
    AX = mybir.AxisListType.X

    P = 128
    B, T, C = x_in.shape
    TILES = B * T // P
    TPB = T // P
    H, G, D = 16, 4, 64
    E, I, K, CAP = 64, 64, 8, 64
    NG, TOPG = 8, 4
    EG = E // NG
    PAIRS = E // 2
    CH = E * TILES // P
    EC = P // TILES
    ROW = C + E
    EPS, NEG = 1e-5, -1e30

    ctx = ExitStack()
    with ctx:
        def sb(name, shape, dt=f32):
            return ctx.enter_context(nc.sbuf_tensor(name, shape, dt))

        def sem(name):
            return ctx.enter_context(nc.semaphore(name))

        NCONST = const_in.shape[1]
        const = sb("const", [P, NCONST])
        at = [0]

        def piece(n):
            at[0] += n
            return const[:, at[0] - n:at[0]]

        ident = piece(P)
        tri_f, before_f, own_f = piece(P), piece(P), piece(EC)
        tile_start, ones_col, slot_no = piece(1), piece(1), piece(1)
        iota = piece(P)
        causal = piece(2 * P)
        rope_q = piece(T)
        cos_k = piece(TPB * 32).rearrange("p (j r) -> p j r", j=TPB)
        sin_k = piece(TPB * 32).rearrange("p (j r) -> p j r", j=TPB)
        nsin_k = piece(TPB * 32).rearrange("p (j r) -> p j r", j=TPB)
        assert at[0] == NCONST
        tri = sb("tri", [P, P], bf16)
        before = sb("before", [P, P], bf16)
        own = sb("own", [P, EC], bf16)
        ext = sb("ext", [P, CH, 3], bf16)

        wq = sb("wq", [P, H, P])
        wkv = sb("wkv", [P, 2 * G * D])
        wo = sb("wo", [P, H * D // P, C])
        w_router = sb("w_router", [P, E])
        w_gu = sb("w_gu", [P, 2, E, I])
        w_down = sb("w_down", [P, PAIRS, C])
        w_sg = sb("w_sg", [P, I])
        w_su = sb("w_su", [P, I])
        w_sd = sb("w_sd", [P, C])

        x = sb("x", [P, TILES, C])
        xn = sb("xn", [P, TILES, C])
        xnT = sb("xnT", [P, TILES * P])
        stats = sb("stats", [P, TILES, 6])
        meanvar = sb("meanvar", [P, TILES, 2])
        std = sb("std", [P, TILES])
        rstd = sb("rstd", [P, TILES])
        bufA = sb("bufA", [P, PAIRS * P])
        bufB = sb("bufB", [P, PAIRS * ROW])
        xgT = bufA[:, :]
        rows = bufB[:, :].rearrange("p (j c) -> p j c", c=ROW)
        onehot = [bufA[:, :].rearrange("p (j t) -> p j t", t=P),
                  bufB[:, 0:PAIRS * P].rearrange("p (j t) -> p j t", t=P)]
        qT = bufA[:, 0:H * T].rearrange("p (h t) -> p h t", t=T)

        scores = sb("scores", [P, TILES, E])
        gmax = sb("gmax", [P, TILES, NG + TOPG])
        gtop = sb("gtop", [P, TILES, 8])
        gleft = sb("gleft", [P, TILES, NG + TOPG])
        gsel = sb("gsel", [P, TILES, NG])
        top = sb("top", [P, TILES, K])
        left = sb("left", [P, TILES, E])
        sel = sb("sel", [P, E, TILES], bf16)
        wsum = sb("wsum", [P, TILES])
        wdense = sb("wdense", [P, TILES, E])
        incl = sb("incl", [P, CH, P], bf16)
        base = sb("base", [P, CH])
        end = sb("end", [P, CH])
        is_from = sb("is_from", [P, CH, CAP], bf16)
        is_to = sb("is_to", [P, CH, CAP], bf16)
        slot_tile = sb("slot_tile", [P, CH, EC, CAP], bf16)
        picked = sb("picked", [P, PAIRS, 3])
        room = sb("room", [P, PAIRS])
        is_le = sb("is_le", [P, PAIRS, P], bf16)
        count = sb("count", [P, PAIRS])
        token = sb("token", [P, PAIRS])
        token_u = sb("token_u", [P, PAIRS], u32)
        wslot = sb("wslot", [P, PAIRS])
        hs = sb("hs", [P, 2, 512])
        hg = sb("hg", [P, 2, 512])
        hT = sb("hT", [P, PAIRS, CAP])
        bufC = sb("bufC", [P, PAIRS * C])
        yw = bufC[:, :].rearrange("p (j c) -> p j c", c=C)
        far = sb("far", [P, 1])
        far1 = sb("far1", [1, 1])
        far_i = sb("far_i", [1, 1], i32)

        xb = sb("xb", [P, T])
        cut = [0]

        def attn(n):
            cut[0] += n
            return bufB[:, cut[0] - n:cut[0]]

        yT = attn(H // 2 * T).rearrange("p (j t) -> p j t", t=T)
        pT = attn(4 * 3 * P).rearrange("p (k t) -> p k t", t=3 * P)
        sm = attn(2 * 3 * P).rearrange("p (k t) -> p k t", t=3 * P)
        kd = attn(TPB * G * 2 * D).rearrange("p (j g a d) -> p j g a d", j=TPB, g=G, a=2)
        n0, n1, n2 = G * T, G * T + TPB * G * D, G * T + TPB * G * D + G * D
        kT = bufC[:, 0:n0].rearrange("p (g t) -> p g t", g=G)
        v = bufC[:, n0:n1].rearrange("p (j n) -> p j n", j=TPB)
        kt1 = bufC[:, n1:n2].rearrange("p (g a r) -> p g a r", g=G, a=2)
        n3 = n2 + G * D
        kt2 = bufC[:, n2:n3].rearrange("p (g a r) -> p g a r", g=G, a=2)
        pr = bufC[:, n3:n3 + 4 * 3 * P].rearrange("p (k t) -> p k t", t=3 * P)
        nmax = sb("nmax", [P, 2, 2])
        rsum = sb("rsum", [P, 4, 2])
        rinv = sb("rinv", [P, 4, 2])

        bank = [ctx.enter_context(nc.psum_tensor(f"bank{i}", [P, 512], f32)) for i in range(8)]
        table = nc.dram_tensor("gather_table", [TILES * P, ROW], f32, kind="Internal").ap()
        table_v = table.rearrange("(i p) c -> p i c", p=P)

        s_const, s_x, s_wr, s_ws, s_wgu, s_wd, s_wa = [sem(n) for n in (
            "const_in", "x_in", "router_in", "shared_in", "gate_up_in", "down_in", "attn_w_in")]
        s_dve = sem("dve_step")
        s_cast = sem("const_cast")
        s_var = sem("variance")
        s_std = sem("std")
        s_xn = sem("xn_group")
        s_xt = sem("xnT_psum")
        s_xnT = sem("xnT")
        s_rt = sem("logits")
        s_sc = sem("scores")
        s_sel = sem("selected")
        s_wdn = sem("dense_weights")
        s_tab = sem("table_stored")
        s_inc = sem("prefix_psum")
        s_incl = sem("prefix")
        s_bas = sem("base_psum")
        s_slt = sem("slot_tile")
        s_pck = sem("picked_psum")
        s_R = sem("prefix_of_slot")
        s_cmp = sem("compared")
        s_tok = sem("token_of_slot")
        s_ga = [sem(f"gathered{i}") for i in range(4)]
        s_xg = sem("xgT_psum")
        s_xgT = sem("xgT")
        s_gu = sem("gate_up_psum")
        s_silu = sem("silu")
        s_h = sem("hidden")
        s_dn = sem("down_psum")
        s_yw = sem("weighted_out")
        s_sgu = sem("shared_gu_psum")
        s_ssilu = sem("shared_silu")
        s_sh = sem("shared_hidden")
        s_sdn = sem("shared_down_psum")
        s_sx = sem("shared_added")
        s_far = sem("last_tile_psum")
        s_fart = sem("last_tile_partial")
        s_far_i = sem("last_tile")
        s_oh = [sem(f"onehot_ffn{n}") for n in range(2)]
        s_cmb = [sem(f"combined_ffn{n}") for n in range(2)]
        s_rel = [sem(f"dve_loop_ffn{n}") for n in range(2)]
        s_done = sem("ffn_done")

        s_xb = sem("xb")
        s_kv = sem("kv_psum")
        s_vsb = sem("v")
        s_kr = sem("k_rope")
        s_ktr = sem("kT_psum")
        s_kt = sem("kT")
        s_qp = sem("q_psum")
        s_qr = sem("q_rope")
        s_qk = sem("scores_psum")
        s_max = sem("row_max")
        s_exp = sem("exp")
        s_nrm = sem("normalised")
        s_tr = sem("pT_psum")
        s_pt = sem("pT")
        s_pv = sem("y_psum")
        s_y = sem("yT")
        s_o = sem("o_psum")
        s_oadd = sem("attn_added")
        s_al = sem("dve_loop_attn")
        s_out = sem("out_stored")

        block = ctx.enter_context(nc.Block())

        @block.sync
        def _(sp):
            sp.dma_start(const[:, :], const_in).then_inc(s_const, 16)
            sp.dma_start(x[:, :, :], x_in.rearrange("b (j p) c -> p (b j) c", p=P)).then_inc(s_x, 16)
            sp.dma_start(w_router[:, :], router_in).then_inc(s_wr, 16)
            sp.dma_start(w_sg[:, :], sg_in).then_inc(s_ws, 16)
            sp.dma_start(w_su[:, :], su_in).then_inc(s_ws, 16)
            sp.dma_start(w_sd[0:I, :], sd_in).then_inc(s_ws, 16)
            sp.dma_start(w_sd[I:P, :], sd_in).then_inc(s_ws, 16)
            sp.dma_start(w_gu[:, :, :, :], gu_in).then_inc(s_wgu, 16)
            sp.dma_start(w_down[:, :, :], down_in).then_inc(s_wd, 16)
            sp.dma_start(wq[:, :, :], wq_in).then_inc(s_wa, 16)
            sp.dma_start(wkv[:, :], wkv_in).then_inc(s_wa, 16)
            sp.dma_start(wo[:, :, :], wo_in.rearrange("(j p) c -> p j c", p=P)).then_inc(s_wa, 16)
            for n in range(2):
                ln = 2 * n
                sp.wait_ge(s_xn, 4 * ln + 4)
                sp.dma_start(table_v[:, :, 0:C], xn[:, :, :]).then_inc(s_tab, 16)
                sp.wait_ge(s_wdn, n + 1)
                sp.dma_start(table_v[:, :, C:ROW], wdense[:, :, :]).then_inc(s_tab, 16)
            sp.wait_ge(s_done, 2)
            sp.dma_start(out.rearrange("b (j p) c -> p (b j) c", p=P), x[:, :, :]).then_inc(s_out, 16)
            sp.wait_ge(s_out, 16)

        @block.gpsimd
        def _(pool):
            for n in range(2):
                pool.wait_ge(s_tok, n + 1)
                pool.wait_ge(s_tab, 32 * (n + 1))
                for j in range(PAIRS):
                    nc.gpsimd.indirect_dma_start(
                        out=rows[:, j, :], out_offset=None, in_=table,
                        in_offset=bass.IndirectOffsetOnAxis(ap=token_u[:, j:j + 1], axis=0),
                    ).then_inc(s_ga[j // 8], 16)

        @block.tensor
        def _(pe):
            mm = nc.tensor.matmul

            def ln_transposes(ln):
                for g in range(4):
                    pe.wait_ge(s_xn, 4 * ln + g + 1)
                    for t in range(4):
                        last = nc.tensor.transpose(bank[g][:, t * P:(t + 1) * P], xn[:, 4 * g + t, :], ident)
                    last.then_inc(s_xt, 1)

            def ffn(n):
                ln = 2 * n
                ln_transposes(ln)
                if n == 0:
                    pe.wait_ge(s_wr, 16)
                for g in range(4):
                    pe.wait_ge(s_xnT, 4 * ln + g + 1)
                    for t in range(4):
                        i = 4 * g + t
                        last = mm(bank[4 + i // 8][:, (i % 8) * E:(i % 8 + 1) * E], xnT[:, i * P:(i + 1) * P],
                                  w_router[:, :], start=True, stop=True)
                    if g % 2:
                        last.then_inc(s_rt, 1)
                if n == 0:
                    pe.wait_ge(s_ws, 64)
                for r in range(2):
                    for w, o in ((w_sg, 0), (w_su, 2)):
                        for half in range(2):
                            last = mm(bank[r + o][half * I:(half + 1) * I, :], w[:, :],
                                      xnT[:, (2 * r + half) * 512:(2 * r + half + 1) * 512], start=True, stop=True)
                    last.then_inc(s_sgu, 1)
                pe.wait_ge(s_sel, n + 1)
                pe.wait_ge(s_sc, 2 * n + 2)
                for c in range(CH):
                    last = mm(bank[4 + c // 4][:, (c % 4) * P:(c % 4 + 1) * P],
                              sel[:, c * EC:(c + 1) * EC, :].rearrange("p e i -> p (e i)"), tri[:, :],
                              start=True, stop=True)
                last.then_inc(s_inc, 1)
                pe.wait_ge(s_incl, n + 1)
                mm(bank[6][:, 0:CH], before[:, :], incl[:, :, P - 1], start=True, stop=True).then_inc(s_bas, 1)
                pe.wait_ge(s_slt, n + 1)
                for j in range(PAIRS):
                    c, q = j // 4, j % 4
                    pair = slot_tile[:, c, 2 * q:2 * q + 2, :].rearrange("p e s -> p (e s)")
                    last = mm(bank[6][:, 64 + 3 * j:67 + 3 * j], pair, ext[:, c, :], start=True, stop=True)
                last.then_inc(s_pck, 1)
                for c in range(CH):
                    if c >= 3:
                        pe.wait_ge(s_cmp, CH * n + c - 2)
                    for q in range(4):
                        pair = slot_tile[:, c, 2 * q:2 * q + 2, :].rearrange("p e s -> p (e s)")
                        last = mm(bank[(4, 5, 7)[c % 3]][:, q * P:(q + 1) * P], pair, incl[:, c, :],
                                  start=True, stop=True)
                    last.then_inc(s_R, 1)
                for g in range(4):
                    pe.wait_ge(s_sh, 2 * n + 2)
                    for t in range(4):
                        half = g % 2
                        last = mm(bank[g][:, t * P:(t + 1) * P],
                                  hs[half * I:(half + 1) * I, g // 2, t * P:(t + 1) * P],
                                  w_sd[half * I:(half + 1) * I, :], start=True, stop=True)
                    last.then_inc(s_sdn, 1)
                if n == 0:
                    pe.wait_ge(s_wgu, 16)
                    pe.wait_ge(s_wd, 16)

                def gate_up(g):
                    for k in range(8):
                        j = 8 * g + k
                        if k % 4 == 0:
                            pe.wait_ge(s_xgT, CH * n + 2 * g + k // 4 + 1)
                        for o in range(2):
                            for e2 in range(2):
                                e = 2 * j + e2
                                last = mm(bank[2 + 2 * (g % 2) + o][e2 * I:(e2 + 1) * I, k * CAP:(k + 1) * CAP],
                                          w_gu[:, o, e, :], xgT[:, e * CAP:(e + 1) * CAP], start=True, stop=True)
                    last.then_inc(s_gu, 1)

                def down(g):
                    pe.wait_ge(s_h, 4 * n + g // 2 + 1)
                    if g >= 2:
                        pe.wait_ge(s_yw, 8 * n + g - 1)
                    for k in range(4):
                        j = 4 * g + k
                        for e2 in range(2):
                            last = mm(bank[6 + g % 2][e2 * CAP:(e2 + 1) * CAP, k * C:(k + 1) * C],
                                      hT[e2 * I:(e2 + 1) * I, j, :], w_down[e2 * I:(e2 + 1) * I, j, :],
                                      start=True, stop=True)
                    last.then_inc(s_dn, 1)

                pe.wait_ge(s_sx, n + 1)
                pe.wait_ge(s_tok, n + 1)
                for g in range(4):
                    pe.wait_ge(s_ga[g], 128 * (n + 1))
                    for k in range(8):
                        q = 2 * g + k // 4
                        if k % 4 == 0 and q >= 2:
                            pe.wait_ge(s_xgT, CH * n + q - 1)
                        last = nc.tensor.transpose(bank[q % 2][:, (k % 4) * P:(k % 4 + 1) * P],
                                                   rows[:, 8 * g + k, 0:C], ident)
                        if k % 4 == 3:
                            last.then_inc(s_xg, 1)
                    if g >= 2:
                        pe.wait_ge(s_h, 4 * n + g - 1)
                    gate_up(g)
                    if g >= 1:
                        down(2 * g - 2)
                        down(2 * g - 1)
                down(6)
                down(7)
                pe.wait_ge(s_fart, n + 1)
                nc.tensor.transpose(bank[2][0:1, 0:P], far[:, :], ident).then_inc(s_far, 1)
                pe.wait_ge(s_yw, 8 * n + 8)
                pe.wait_ge(s_far_i, n + 1)
                last_tile = pe.value_load(far_i[0:1, 0:1], min_val=0, max_val=(TILES - 1) * P)
                with pe.Fori(0, TILES // 2) as it:
                    with pe.If(it * (2 * P) <= last_tile):
                        for u in range(2):
                            pe.wait_ge(s_oh[n], it * 2 + (u + 1))
                            for j in range(PAIRS):
                                last = mm(bank[u][:, 0:C], onehot[u][:, j, :], yw[:, j, :],
                                          start=(j == 0), stop=(j == PAIRS - 1))
                            last.then_inc(s_cmb[n], 1)

            def attention():
                ln_transposes(1)
                pe.wait_ge(s_wa, 48)

                def q_proj(b, p):
                    pe.wait_ge(s_qr, b * 8 + max(p - 1, 0))
                    for k in range(2):
                        last = mm(bank[2 + p % 2][:, k * T:(k + 1) * T], wq[:, 2 * p + k, :], xb[:, :],
                                  start=True, stop=True)
                    last.then_inc(s_qp, 1)

                with pe.Fori(0, B) as b:
                    pe.wait_ge(s_xb, b + 1)
                    for j in range(TPB):
                        mm(bank[4 + j][:, :], xb[:, j * P:(j + 1) * P], wkv[:, :], start=True, stop=True)\
                            .then_inc(s_kv, 1)
                    q_proj(b, 0)
                    q_proj(b, 1)
                    for j in range(TPB):
                        pe.wait_ge(s_kr, b * 2 + (j + 1))
                        for g in range(G):
                            last = nc.tensor.transpose(bank[j][:, g * P:(g + 1) * P],
                                                       kd[:, j, g, :, :].rearrange("p a d -> p (a d)"), ident)
                        last.then_inc(s_ktr, 1)
                    pe.wait_ge(s_vsb, b * 2 + 2)
                    pe.wait_ge(s_kt, b * 2 + 2)
                    for h in range(H + 3):
                        if h < 2:
                            q_proj(b, h + 2)
                        if h < H:
                            pe.wait_ge(s_qr, b * 8 + (h // 2 + 1))
                            if h >= 2:
                                pe.wait_ge(s_max, b * H + (h - 1))
                            mm(bank[h % 2][:, 0:P], qT[:, h, 0:P], kT[:, h // (H // G), 0:P], start=True, stop=True)
                            mm(bank[h % 2][:, P:3 * P], qT[:, h, P:T], kT[:, h // (H // G), :],
                               start=True, stop=True).then_inc(s_qk, 1)
                        if h in (2, 4, 6, 8):
                            q_proj(b, h // 2 + 3)
                        if 2 <= h < H + 2:
                            k = h - 2
                            pe.wait_ge(s_nrm, b * H + (k + 1))
                            if k >= 2:
                                pe.wait_ge(s_pt, b * H + (k - 1))
                            for t in range(3):
                                last = nc.tensor.transpose(bank[4 + k % 2][:, t * P:(t + 1) * P],
                                                           pr[:, k % 4, t * P:(t + 1) * P], ident)
                            last.then_inc(s_tr, 1)
                        if h >= 4 and h % 2 == 0:
                            p = (h - 4) // 2
                            pe.wait_ge(s_pt, b * H + (2 * p + 2))
                            if p >= 1:
                                pe.wait_ge(s_y, b * 8 + p)
                            g = 2 * p // (H // G)
                            for kt in range(2):
                                for k in range(2):
                                    o = bank[6][k * D:(k + 1) * D, :]
                                    q = pT[:, (2 * p + k) % 4, :]
                                    last = mm(o[:, 0:T] if kt == 0 else o[:, P:T],
                                              v[:, kt, g * D:(g + 1) * D], q[:, 0:T] if kt == 0 else q[:, T:3 * P],
                                              start=(kt == 0), stop=(kt == 1))
                            last.then_inc(s_pv, 1)
                    pe.wait_ge(s_y, b * 8 + 8)
                    for j in range(TPB):
                        for p in range(H // 2):
                            last = mm(bank[7][:, j * C:(j + 1) * C], yT[:, p, j * P:(j + 1) * P], wo[:, p, :],
                                      start=(p == 0), stop=(p == H // 2 - 1))
                    last.then_inc(s_o, 1)
                    pe.wait_ge(s_oadd, b + 1)

            pe.wait_ge(s_const, 16)
            pe.wait_ge(s_cast, 3)
            ffn(0)
            attention()
            ffn(1)

        @block.scalar
        def _(act):
            def layernorm(ln):
                act.wait_ge(s_var, ln + 1)
                nc.scalar.activation(std[:, :], std[:, :], ACT.Sqrt).then_inc(s_std, 1)
                for g in range(4):
                    act.wait_ge(s_xt, 4 * ln + g + 1)
                    nc.scalar.copy(xnT[:, g * 512:(g + 1) * 512], bank[g][:, :]).then_inc(s_xnT, 1)

            def ffn(n):
                layernorm(2 * n)
                for r in range(2):
                    act.wait_ge(s_rt, 2 * n + r + 1)
                    nc.scalar.activation(scores[:, 8 * r:8 * r + 8, :], bank[4 + r][:, :], ACT.Sigmoid)\
                        .then_inc(s_sc, 1)
                for r in range(2):
                    act.wait_ge(s_sgu, 2 * n + r + 1)
                    nc.scalar.activation(hs[:, r, :], bank[r][:, :], ACT.Silu).then_inc(s_ssilu, 1)
                act.wait_ge(s_inc, n + 1)
                nc.scalar.copy(incl[:, 0:4, :], bank[4][:, :])
                nc.scalar.copy(incl[:, 4:8, :], bank[5][:, :]).then_inc(s_incl, 1)

                def silu(g):
                    act.wait_ge(s_gu, 4 * n + g + 1)
                    if g >= 2:
                        act.wait_ge(s_h, 4 * n + g - 1)
                    nc.scalar.activation(hg[:, g % 2, :], bank[2 + 2 * (g % 2)][:, :], ACT.Silu).then_inc(s_silu, 1)

                for g in range(8):
                    act.wait_ge(s_xg, 8 * n + g + 1)
                    nc.scalar.copy(xgT[:, g * 512:(g + 1) * 512], bank[g % 2][:, :]).then_inc(s_xgT, 1)
                    if g % 2:
                        silu(g // 2)

            def attention():
                layernorm(1)
                act.wait_ge(s_xnT, 8)
                with act.Fori(0, B) as b:
                    act.wait_ge(s_qp, b * 8)
                    act.wait_ge(s_kv, b * 2)
                    nc.scalar.copy(xb[:, :], xnT[:, bass.ds(b * T, T)]).then_inc(s_xb, 1)
                    act.wait_ge(s_pv, b * 8)
                    for j in range(TPB):
                        act.wait_ge(s_kv, b * 2 + (j + 1))
                        nc.scalar.copy(v[:, j, :], bank[4 + j][:, G * D:2 * G * D]).then_inc(s_vsb, 1)
                    for h in range(H + 5):
                        if h < H:
                            act.wait_ge(s_max, b * H + (h + 1))
                            act.wait_ge(s_tr, b * H + max(h - 3, 0))
                            k, r = h % 2, h % 4
                            nc.scalar.activation(pr[:, r, 0:P], sm[:, k, 0:P], ACT.Exp, bias=nmax[:, k, 0:1],
                                                 scale=-1.0, accum_out=rsum[:, r, 0:1])
                            nc.scalar.activation(pr[:, r, P:3 * P], sm[:, k, P:3 * P], ACT.Exp, bias=nmax[:, k, 1:2],
                                                 scale=-1.0, accum_out=rsum[:, r, 1:2]).then_inc(s_exp, 1)
                        if 3 <= h <= H + 2:
                            k = h - 3
                            act.wait_ge(s_tr, b * H + (k + 1))
                            if k >= 4:
                                act.wait_ge(s_pv, b * 8 + (k // 2 - 1))
                            nc.scalar.copy(pT[:, k % 4, :], bank[4 + k % 2][:, 0:3 * P]).then_inc(s_pt, 1)
                        if h >= 6 and h % 2 == 0:
                            p = (h - 6) // 2
                            act.wait_ge(s_pv, b * 8 + (p + 1))
                            nc.scalar.copy(yT[:, p, :], bank[6][:, 0:T]).then_inc(s_y, 1)

            ffn(0)
            attention()
            ffn(1)

        @block.vector
        def _(dve):
            vec = nc.vector
            steps = [0]

            def step(ins):
                steps[0] += 1
                ins.then_inc(s_dve, 1)
                dve.wait_ge(s_dve, steps[0])

            def layernorm(ln):
                for i in range(TILES):
                    last = vec.bn_stats(stats[:, i, :], x[:, i, :])
                step(last)
                for i in range(TILES):
                    last = vec.bn_aggr(meanvar[:, i, :], stats[:, i, :])
                step(last)
                vec.tensor_scalar(std[:, :], meanvar[:, :, 1], EPS, None, ALU.add).then_inc(s_var, 1)
                dve.wait_ge(s_std, ln + 1)
                step(vec.reciprocal(rstd[:, :], std[:, :]))
                if ln == 2:
                    dve.wait_ge(s_tab, 32)
                for i in range(TILES):
                    last = vec.tensor_scalar(xn[:, i, :], x[:, i, :], meanvar[:, i, 0:1], rstd[:, i:i + 1],
                                             ALU.subtract, ALU.mult)
                    if i % 4 == 3:
                        last.then_inc(s_xn, 1)

            def choose(n):
                dve.wait_ge(s_sc, 2 * n + 2)
                sc4 = scores[:, :, :].rearrange("p i (g e) -> p i g e", g=NG)
                step(vec.tensor_reduce(gmax[:, :, 0:NG], sc4, AX, ALU.max))
                for i in range(TILES):
                    last = vec.max(gtop[:, i, :], gmax[:, i, 0:NG])
                step(last)
                step(vec.memset(gtop[:, :, TOPG:8], -1.0))
                for i in range(TILES):
                    last = vec.match_replace(gleft[:, i, :], gtop[:, i, :], gmax[:, i, :], 2.0)
                step(last)
                step(vec.tensor_scalar(gsel[:, :, :], gleft[:, :, 0:NG], 1.5, None, ALU.is_gt))
                step(vec.tensor_tensor(sc4, sc4, gsel[:, :, :].unsqueeze(3).to_broadcast([P, TILES, NG, EG]), ALU.mult))
                for i in range(TILES):
                    last = vec.max(top[:, i, :], scores[:, i, :])
                step(last)
                for i in range(TILES):
                    last = vec.match_replace(left[:, i, :], top[:, i, :], scores[:, i, :], -1.0)
                step(last)
                vec.tensor_scalar(sel[:, :, :].rearrange("p e i -> p i e"), left[:, :, :], 0.0, None, ALU.is_lt)\
                    .then_inc(s_sel, 1)
                step(vec.tensor_reduce(wsum[:, :], top[:, :, :], AX, ALU.add))
                step(vec.tensor_scalar(wsum[:, :], wsum[:, :], 1e-9, None, ALU.max))
                step(vec.reciprocal(wsum[:, :], wsum[:, :]))
                step(vec.tensor_scalar(wsum[:, :], wsum[:, :], 1.25, None, ALU.mult))
                if n == 1:
                    dve.wait_ge(s_tab, 32)
                step(vec.scalar_tensor_tensor(out=wdense[:, :, :], in0=left[:, :, :], scalar=0.0,
                                              in1=scores[:, :, :], op0=ALU.is_lt, op1=ALU.mult))
                vec.tensor_tensor(wdense[:, :, :], wdense[:, :, :], wsum[:, :].unsqueeze(2).to_broadcast([P, TILES, E]),
                                  ALU.mult).then_inc(s_wdn, 1)

            def slots(n):
                dve.wait_ge(s_bas, n + 1)
                vec.tensor_copy(base[:, :], bank[6][:, 0:CH])
                vec.tensor_copy(ext[:, :, 0], bank[6][:, 0:CH])
                step(vec.tensor_tensor(end[:, :], bank[6][:, 0:CH], incl[:, :, P - 1], ALU.add))
                io = iota[:, 0:CAP].unsqueeze(1).to_broadcast([P, CH, CAP])
                vec.tensor_tensor(is_from[:, :, :], io, base[:, :].unsqueeze(2).to_broadcast([P, CH, CAP]), ALU.is_ge)
                step(vec.tensor_tensor(is_to[:, :, :], io, end[:, :].unsqueeze(2).to_broadcast([P, CH, CAP]), ALU.is_lt))
                step(vec.tensor_tensor(is_from[:, :, :], is_from[:, :, :], is_to[:, :, :], ALU.mult))
                vec.tensor_tensor(slot_tile[:, :, :, :],
                                  is_from[:, :, :].unsqueeze(2).to_broadcast([P, CH, EC, CAP]),
                                  own[:, :].unsqueeze(1).unsqueeze(3).to_broadcast([P, CH, EC, CAP]),
                                  ALU.mult).then_inc(s_slt, 1)
                dve.wait_ge(s_pck, n + 1)
                step(vec.tensor_copy(picked[:, :, :], bank[6][:, 64:64 + 3 * PAIRS]))
                step(vec.scalar_tensor_tensor(out=room[:, :], in0=picked[:, :, 0], scalar=-1.0,
                                              in1=slot_no.to_broadcast([P, PAIRS]), op0=ALU.mult, op1=ALU.add))
                for c in range(CH):
                    dve.wait_ge(s_R, CH * n + c + 1)
                    vec.tensor_tensor(is_le[:, 4 * c:4 * c + 4, :],
                                      bank[(4, 5, 7)[c % 3]][:, :].rearrange("p (j t) -> p j t", t=P),
                                      room[:, 4 * c:4 * c + 4].unsqueeze(2).to_broadcast([P, 4, P]),
                                      ALU.is_le).then_inc(s_cmp, 1)
                dve.wait_ge(s_cmp, CH * (n + 1))
                step(vec.tensor_reduce(count[:, :], is_le[:, :, :], AX, ALU.add))
                step(vec.tensor_tensor(token[:, :], count[:, :], picked[:, :, 1], ALU.add))
                vec.tensor_copy(token_u[:, :], token[:, :]).then_inc(s_tok, 1)
                vec.tensor_reduce(far[:, :], picked[:, :, 1], AX, ALU.max).then_inc(s_fart, 1)

            def shared(n):
                for r in range(2):
                    dve.wait_ge(s_ssilu, 2 * n + r + 1)
                    vec.tensor_tensor(hs[:, r, :], hs[:, r, :], bank[2 + r][:, :], ALU.mult).then_inc(s_sh, 1)

            def shared_add(n):
                for g in range(4):
                    dve.wait_ge(s_sdn, 4 * n + g + 1)
                    last = vec.scalar_tensor_tensor(
                        out=x[:, 4 * g:4 * g + 4, :], in0=bank[g][:, :].rearrange("p (i c) -> p i c", c=C), scalar=0.5,
                        in1=x[:, 4 * g:4 * g + 4, :], op0=ALU.mult, op1=ALU.add)
                last.then_inc(s_sx, 1)

            def experts(n):
                for g in range(4):
                    dve.wait_ge(s_ga[g], 128 * (n + 1))
                for e2 in range(2):
                    q = slice(e2 * CAP, (e2 + 1) * CAP)
                    w = bufB[q, C + e2:C + e2 + (PAIRS - 1) * (ROW + 2) + 1:ROW + 2]
                    last = vec.tensor_tensor(wslot[q, :], w, picked[q, :, 2], ALU.mult)
                step(last)
                for g in range(8):
                    if g % 2 == 0:
                        dve.wait_ge(s_silu, 4 * n + g // 2 + 1)
                        dve.wait_ge(s_gu, 4 * n + g // 2 + 1)
                        vec.tensor_tensor(hT[:, 4 * g:4 * g + 8, :], hg[:, (g // 2) % 2, :].rearrange("p (j s) -> p j s", s=CAP),
                                          bank[3 + 2 * ((g // 2) % 2)][:, :].rearrange("p (j s) -> p j s", s=CAP),
                                          ALU.mult).then_inc(s_h, 1)
                    dve.wait_ge(s_dn, 8 * n + g + 1)
                    vec.tensor_tensor(yw[:, 4 * g:4 * g + 4, :], bank[6 + g % 2][:, :].rearrange("p (j c) -> p j c", c=C),
                                      wslot[:, 4 * g:4 * g + 4].unsqueeze(2).to_broadcast([P, 4, C]),
                                      ALU.mult).then_inc(s_yw, 1)
                dve.wait_ge(s_far, n + 1)
                step(vec.tensor_reduce(far1[:, :], bank[2][0:1, 0:P], AX, ALU.max))
                vec.tensor_copy(far_i[:, :], far1[:, :]).then_inc(s_far_i, 1)

            def combine(n):
                dve.wait_ge(s_far_i, n + 1)
                last_tile = dve.value_load(far_i[0:1, 0:1], min_val=0, max_val=(TILES - 1) * P)
                with dve.Fori(0, TILES // 2) as it:
                    with dve.If(it * (2 * P) <= last_tile):
                        for u in range(2):
                            dve.wait_ge(s_rel[n], it * 2 + u)
                            dve.wait_ge(s_cmb[n], it * 2)
                            vec.tensor_tensor(onehot[u], iota.unsqueeze(1).to_broadcast([P, PAIRS, P]),
                                              token[:, :].unsqueeze(2).to_broadcast([P, PAIRS, P]),
                                              ALU.is_equal).then_inc(s_oh[n], 1)
                            dve.wait_ge(s_oh[n], it * 2 + (u + 1))
                            vec.tensor_scalar(token[:, :], token[:, :], -float(P), None, ALU.add).then_inc(s_rel[n], 1)
                        for u in range(2):
                            dve.wait_ge(s_cmb[n], it * 2 + (u + 1))
                            vec.tensor_tensor(x[:, bass.ds(it * 2 + u, 1), :], x[:, bass.ds(it * 2 + u, 1), :],
                                              bank[u][:, 0:C].unsqueeze(1), ALU.add)
                step(vec.memset(far1[:, :], 0.0))
                vec.memset(far1[:, :], 0.0).then_inc(s_done, 1)

            def ffn(n):
                layernorm(2 * n)
                choose(n)
                shared(n)
                slots(n)
                shared_add(n)
                experts(n)
                combine(n)

            def attention():
                layernorm(1)

                def q_rope(b, p):
                    dve.wait_ge(s_qp, b * 8 + (p + 1))
                    vec.tensor_tensor(qT[:, 2 * p:2 * p + 2, :], bank[2 + p % 2][:, :].rearrange("p (h t) -> p h t", t=T),
                                      rope_q.unsqueeze(1).to_broadcast([P, 2, T]), ALU.mult).then_inc(s_qr, 1)

                with dve.Fori(0, B) as b:
                    for j in range(TPB):
                        dve.wait_ge(s_vsb, b * 2 + (j + 1))
                        k = bank[4 + j][:, 0:G * D].rearrange("p (g a r) -> p g a r", g=G, a=2)
                        r3 = [P, G, 32]
                        dve.wait_ge(s_kr, b * 2 + j)
                        vec.tensor_tensor(kt1[:, :, :, :], k, cos_k[:, j, :].unsqueeze(1).unsqueeze(1).to_broadcast([P, G, 2, 32]), ALU.mult)
                        vec.tensor_tensor(kt2[:, :, 0, :], k[:, :, 1, :], nsin_k[:, j, :].unsqueeze(1).to_broadcast(r3), ALU.mult)
                        vec.tensor_tensor(kt2[:, :, 1, :], k[:, :, 0, :], sin_k[:, j, :].unsqueeze(1).to_broadcast(r3), ALU.mult)\
                            .then_inc(s_al, 1)
                        dve.wait_ge(s_al, b * 18 + (j + 1))
                        for a in range(2):
                            last = vec.tensor_tensor(kd[:, j, :, a, :], kt1[:, :, :, :].rearrange("p g a r -> p g (a r)"),
                                                     kt2[:, :, :, :].rearrange("p g a r -> p g (a r)"), ALU.add)
                        last.then_inc(s_kr, 1)
                    q_rope(b, 0)
                    q_rope(b, 1)
                    for j in range(TPB):
                        dve.wait_ge(s_ktr, b * 2 + (j + 1))
                        vec.tensor_copy(kT[:, :, j * P:(j + 1) * P], bank[j][:, :].rearrange("p (g t) -> p g t", g=G))\
                            .then_inc(s_kt, 1)
                    for h in range(H + 2):
                        if h < H:
                            dve.wait_ge(s_qk, b * H + (h + 1))
                        if h < 2:
                            q_rope(b, h + 2)
                        else:
                            r = (h - 2) % 4
                            dve.wait_ge(s_exp, b * H + (h - 1))
                            vec.reciprocal(rinv[:, r, :], rsum[:, r, :]).then_inc(s_al, 1)
                            dve.wait_ge(s_al, b * 18 + (1 + h))
                            vec.tensor_scalar(pr[:, r, 0:P], pr[:, r, 0:P], rinv[:, r, 0:1], None, ALU.mult)
                            vec.tensor_scalar(pr[:, r, P:3 * P], pr[:, r, P:3 * P], rinv[:, r, 1:2], None, ALU.mult)\
                                .then_inc(s_nrm, 1)
                        if h < H:
                            k = h % 2
                            vec.tensor_tensor_reduce(out=sm[:, k, 0:P], in0=bank[k][:, 0:P], in1=causal[:, P:2 * P],
                                                     scale=-0.125, scalar=3e38, op0=ALU.add, op1=ALU.min,
                                                     accum_out=nmax[:, k, 0:1])
                            vec.tensor_tensor_reduce(out=sm[:, k, P:3 * P], in0=bank[k][:, P:3 * P], in1=causal,
                                                     scale=-0.125, scalar=3e38, op0=ALU.add, op1=ALU.min,
                                                     accum_out=nmax[:, k, 1:2]).then_inc(s_max, 1)
                        if h in (2, 4, 6, 8):
                            q_rope(b, h // 2 + 3)
                    dve.wait_ge(s_o, b + 1)
                    vec.tensor_tensor(x[:, bass.ds(b * TPB, TPB), :], x[:, bass.ds(b * TPB, TPB), :],
                                      bank[7][:, 0:TPB * C].rearrange("p (j c) -> p j c", c=C), ALU.add)\
                        .then_inc(s_oadd, 1)

            dve.wait_ge(s_const, 16)
            vec.tensor_copy(tri[:, :], tri_f).then_inc(s_cast, 1)
            vec.tensor_copy(before[:, :], before_f).then_inc(s_cast, 1)
            vec.tensor_copy(own[:, :], own_f).then_inc(s_cast, 1)
            vec.tensor_copy(ext[:, :, 1], tile_start.to_broadcast([P, CH]))
            vec.tensor_copy(ext[:, :, 2], ones_col.to_broadcast([P, CH]))
            step(vec.memset(gmax[:, :, NG:], -1.0))
            dve.wait_ge(s_x, 16)
            ffn(0)
            dve.wait_ge(s_done, 1)
            attention()
            dve.wait_ge(s_oadd, B)
            ffn(1)


def shape_constants(np):
    P, T, TILES, EC = 128, 256, 16, 8
    p = np.arange(P)[:, None]
    q = np.arange(P)[None, :]
    inv_freq = (1.0 / np.float32(10000.0) ** (np.arange(0, 64, 2, dtype=np.float32) / np.float32(64))).astype(np.float32)
    angle = (np.arange(T, dtype=np.float32)[:, None] * inv_freq[None, :]).astype(np.float32)
    cos, sin = np.cos(angle), np.sin(angle)
    ck = cos.reshape(2, P, 32).transpose(1, 0, 2).reshape(P, 64)
    sk = sin.reshape(2, P, 32).transpose(1, 0, 2).reshape(P, 64)
    parts = [
        p == q,
        p <= q,
        (p // TILES == q // TILES) & (p < q),
        p // TILES == np.arange(EC)[None, :],
        p % TILES * P,
        np.ones((P, 1)),
        p % 64,
        np.zeros((P, 1)) + q,
        np.zeros((P, P)), np.where(q <= p, 0.0, -1e30),
        np.concatenate([cos, cos, -sin, sin], axis=1).T,
        ck, sk, -sk,
    ]
    return np.ascontiguousarray(np.concatenate([a.astype(np.float32) for a in parts], axis=1))


def kernel(**inputs):
    import numpy as np
    import concourse.bacc as bacc
    from concourse.bass_utils import run_bass_kernel_spmd

    a = {n[3:]: np.asarray(v) for n, v in inputs.items()}
    wq = a["attn_Wq"].reshape(128, 16, 32, 2)
    even, odd = wq[..., 0], wq[..., 1]
    wk = a["attn_Wk"].reshape(128, 4, 32, 2)
    arrays = {
        "x": a["attn_x"],
        "wq": np.concatenate([even, odd, odd, even], axis=2),
        "wkv": np.concatenate([wk.transpose(0, 1, 3, 2).reshape(128, 256), a["attn_Wv"]], axis=1),
        "wo": a["attn_Wo"],
        "router": a["ffn_router_w"],
        "gate_up": np.stack([a["ffn_gate_w"].transpose(1, 0, 2), a["ffn_up_w"].transpose(1, 0, 2)], axis=1),
        "down": a["ffn_down_w"].reshape(32, 128, 128).transpose(1, 0, 2),
        "shared_gate": a["ffn_shared_gate_w"],
        "shared_up": a["ffn_shared_up_w"],
        "shared_down": a["ffn_shared_down_w"],
        "shape_constants": shape_constants(np),
    }
    arrays = {n: np.ascontiguousarray(v) for n, v in arrays.items()}
    nc = bacc.Bacc("TRN2", target_bir_lowering=False, num_devices=1)
    args = [nc.dram_tensor(f"{n}_dram", v.shape, mybir.dt.from_np(v.dtype), kind="ExternalInput").ap() for n, v in arrays.items()]
    args.append(nc.dram_tensor("result", (8, 256, 128), mybir.dt.float32, kind="ExternalOutput").ap())
    macaron_block(nc, *args)
    r = run_bass_kernel_spmd(nc, [{f"{n}_dram": v for n, v in arrays.items()}], core_ids=[0])
    return r.results[0]["result"]
```

```python
import concourse.bass as bass
from concourse import mybir
from contextlib import ExitStack


def macaron_block(nc, x_in, wq_in, wkv_in, wo_in, router_in, gu_in, down_in, sg_in, su_in, sd_in, const_in, out):
    f32 = mybir.dt.float32
    bf16 = mybir.dt.bfloat16
    u32 = mybir.dt.uint32
    i32 = mybir.dt.int32
    ALU = mybir.AluOpType
    ACT = mybir.ActivationFunctionType
    AX = mybir.AxisListType.X

    P = 128
    B, T, C = x_in.shape
    TILES = B * T // P
    TPB = T // P
    H, G, D = 16, 4, 64
    E, I, K, CAP = 64, 64, 8, 64
    NG, TOPG = 8, 4
    EG = E // NG
    PAIRS = E // 2
    CH = E * TILES // P
    EC = P // TILES
    ROW = C + E
    EPS, NEG = 1e-5, -1e30

    ctx = ExitStack()
    with ctx:
        def sb(name, shape, dt=f32):
            return ctx.enter_context(nc.sbuf_tensor(name, shape, dt))

        def sem(name):
            return ctx.enter_context(nc.semaphore(name))

        NCONST = const_in.shape[1]
        const = sb("const", [P, NCONST])
        at = [0]

        def piece(n):
            at[0] += n
            return const[:, at[0] - n:at[0]]

        ident = piece(P)
        tri_f, before_f, own_f = piece(P), piece(P), piece(EC)
        tile_start, ones_col, slot_no = piece(1), piece(1), piece(1)
        iota = piece(P)
        causal = piece(2 * P)
        rope_q = piece(T)
        cos_k = piece(TPB * 32).rearrange("p (j r) -> p j r", j=TPB)
        sin_k = piece(TPB * 32).rearrange("p (j r) -> p j r", j=TPB)
        nsin_k = piece(TPB * 32).rearrange("p (j r) -> p j r", j=TPB)
        assert at[0] == NCONST
        tri = sb("tri", [P, P], bf16)
        before = sb("before", [P, P], bf16)
        own = sb("own", [P, EC], bf16)
        ext = sb("ext", [P, CH, 3], bf16)

        wq = sb("wq", [P, H, P])
        wkv = sb("wkv", [P, 2 * G * D])
        wo = sb("wo", [P, H * D // P, C])
        w_router = sb("w_router", [P, E])
        w_gu = sb("w_gu", [P, 2, E, I])
        w_down = sb("w_down", [P, PAIRS, C])
        w_sg = sb("w_sg", [P, I])
        w_su = sb("w_su", [P, I])
        w_sd = sb("w_sd", [P, C])

        x = sb("x", [P, TILES, C])
        xn = sb("xn", [P, TILES, C])
        xnT = sb("xnT", [P, TILES * P])
        stats = sb("stats", [P, TILES, 6])
        meanvar = sb("meanvar", [P, TILES, 2])
        std = sb("std", [P, TILES])
        rstd = sb("rstd", [P, TILES])
        bufA = sb("bufA", [P, PAIRS * P])
        bufB = sb("bufB", [P, PAIRS * ROW])
        xgT = bufA[:, :]
        rows = bufB[:, :].rearrange("p (j c) -> p j c", c=ROW)
        onehot = [bufA[:, :].rearrange("p (j t) -> p j t", t=P),
                  bufB[:, 0:PAIRS * P].rearrange("p (j t) -> p j t", t=P)]
        qT = bufA[:, 0:H * T].rearrange("p (h t) -> p h t", t=T)

        scores = sb("scores", [P, TILES, E])
        gmax = sb("gmax", [P, TILES, NG + TOPG])
        gtop = sb("gtop", [P, TILES, 8])
        gleft = sb("gleft", [P, TILES, NG + TOPG])
        gsel = sb("gsel", [P, TILES, NG])
        top = sb("top", [P, TILES, K])
        left = sb("left", [P, TILES, E])
        sel = sb("sel", [P, E, TILES], bf16)
        wsum = sb("wsum", [P, TILES])
        wdense = sb("wdense", [P, TILES, E])
        incl = sb("incl", [P, CH, P], bf16)
        base = sb("base", [P, CH])
        end = sb("end", [P, CH])
        is_from = sb("is_from", [P, CH, CAP], bf16)
        is_to = sb("is_to", [P, CH, CAP], bf16)
        slot_tile = sb("slot_tile", [P, CH, EC, CAP], bf16)
        picked = sb("picked", [P, PAIRS, 3])
        room = sb("room", [P, PAIRS])
        is_le = sb("is_le", [P, PAIRS, P], bf16)
        count = sb("count", [P, PAIRS])
        token = sb("token", [P, PAIRS])
        token_u = sb("token_u", [P, PAIRS], u32)
        wslot = sb("wslot", [P, PAIRS])
        hs = sb("hs", [P, 2, 512])
        hg = sb("hg", [P, 2, 512])
        hT = sb("hT", [P, PAIRS, CAP])
        bufC = sb("bufC", [P, PAIRS * C])
        yw = bufC[:, :].rearrange("p (j c) -> p j c", c=C)
        far = sb("far", [P, 1])
        far1 = sb("far1", [1, 1])
        far_i = sb("far_i", [1, 1], i32)

        xb = sb("xb", [P, T])
        kvn = hT[:, 0:TPB * 2 * G * D // CAP, :].rearrange("p j c -> p (j c)").rearrange("p (j n) -> p j n", j=TPB)
        cut = [0]

        def attn(n):
            cut[0] += n
            return bufB[:, cut[0] - n:cut[0]]

        yT = attn(H // 2 * T).rearrange("p (j t) -> p j t", t=T)
        pT = attn(4 * 3 * P).rearrange("p (k t) -> p k t", t=3 * P)
        sm = attn(2 * 3 * P).rearrange("p (k t) -> p k t", t=3 * P)
        kd = attn(TPB * G * 2 * D).rearrange("p (j g a d) -> p j g a d", j=TPB, g=G, a=2)
        n0, n1, n2 = G * T, G * T + TPB * G * D, G * T + TPB * G * D + G * D
        kT = bufC[:, 0:n0].rearrange("p (g t) -> p g t", g=G)
        v = bufC[:, n0:n1].rearrange("p (j n) -> p j n", j=TPB)
        kt1 = bufC[:, n1:n2].rearrange("p (g a r) -> p g a r", g=G, a=2)
        n3 = n2 + G * D
        kt2 = bufC[:, n2:n3].rearrange("p (g a r) -> p g a r", g=G, a=2)
        pr = bufC[:, n3:n3 + 4 * 3 * P].rearrange("p (k t) -> p k t", t=3 * P)
        nmax = sb("nmax", [P, 2, 2])
        rsum = sb("rsum", [P, 4, 2])
        rinv = sb("rinv", [P, 4, 2])

        bank = [ctx.enter_context(nc.psum_tensor(f"bank{i}", [P, 512], f32)) for i in range(8)]
        table = nc.dram_tensor("gather_table", [TILES * P, ROW], f32, kind="Internal").ap()
        table_v = table.rearrange("(i p) c -> p i c", p=P)

        s_const, s_x, s_wr, s_ws, s_wgu, s_wd, s_wa = [sem(n) for n in (
            "const_in", "x_in", "router_in", "shared_in", "gate_up_in", "down_in", "attn_w_in")]
        s_dve = sem("dve_step")
        s_cast = sem("const_cast")
        s_var = sem("variance")
        s_std = sem("std")
        s_xn = sem("xn_group")
        s_xt = sem("xnT_psum")
        s_xnT = sem("xnT")
        s_rt = sem("logits")
        s_sc = sem("scores")
        s_sel = sem("selected")
        s_wdn = sem("dense_weights")
        s_tab = sem("table_stored")
        s_inc = sem("prefix_psum")
        s_incl = sem("prefix")
        s_bas = sem("base_psum")
        s_slt = sem("slot_tile")
        s_pck = sem("picked_psum")
        s_R = sem("prefix_of_slot")
        s_cmp = sem("compared")
        s_tok = sem("token_of_slot")
        s_ga = [sem(f"gathered{i}") for i in range(4)]
        s_xg = sem("xgT_psum")
        s_xgT = sem("xgT")
        s_gu = sem("gate_up_psum")
        s_silu = sem("silu")
        s_h = sem("hidden")
        s_dn = sem("down_psum")
        s_yw = sem("weighted_out")
        s_sgu = sem("shared_gu_psum")
        s_ssilu = sem("shared_silu")
        s_sh = sem("shared_hidden")
        s_sdn = sem("shared_down_psum")
        s_sx = sem("shared_added")
        s_far = sem("last_tile_psum")
        s_fart = sem("last_tile_partial")
        s_far_i = sem("last_tile")
        s_oh = [sem(f"onehot_ffn{n}") for n in range(2)]
        s_cmb = [sem(f"combined_ffn{n}") for n in range(2)]
        s_rel = [sem(f"dve_loop_ffn{n}") for n in range(2)]
        s_done = sem("ffn_done")

        s_xb = sem("xb")
        s_kv = sem("kv_psum")
        s_kvn = sem("kv_next")
        s_v = sem("v")
        s_kpart = sem("k_rope_parts")
        s_rinv = sem("row_sum_inverse")
        s_kr = sem("k_rope")
        s_ktr = sem("kT_psum")
        s_kt = sem("kT")
        s_qp = sem("q_psum")
        s_qr = sem("q_rope")
        s_qk = sem("scores_psum")
        s_max = sem("row_max")
        s_exp = sem("exp")
        s_nrm = sem("normalised")
        s_tr = sem("pT_psum")
        s_pt = sem("pT")
        s_pv = sem("y_psum")
        s_y = sem("yT")
        s_o = sem("o_psum")
        s_oadd = sem("attn_added")
        s_out = sem("out_stored")

        def wait(eng, s, count):
            if not isinstance(count, int) or count > 0:
                eng.wait_ge(s, count)

        HB = H // 2
        Q_AT = {1: (1, 2), 2: (2, 3), 4: (3, 2), 5: (4, 3), 7: (5, 3), 9: (6, 3), 11: (7, 2)}
        KV_AT, Q0_AT, KT_AT = (6, 8), 12, (13, 14)
        Q_BANK = {p: n for p, n in Q_AT.values()} | {0: 3}

        block = ctx.enter_context(nc.Block())

        @block.sync
        def _(sp):
            sp.dma_start(const[:, :], const_in).then_inc(s_const, 16)
            sp.dma_start(x[:, :, :], x_in.rearrange("b (j p) c -> p (b j) c", p=P)).then_inc(s_x, 16)
            sp.dma_start(w_router[:, :], router_in).then_inc(s_wr, 16)
            sp.dma_start(w_sg[:, :], sg_in).then_inc(s_ws, 16)
            sp.dma_start(w_su[:, :], su_in).then_inc(s_ws, 16)
            sp.dma_start(w_sd[0:I, :], sd_in).then_inc(s_ws, 16)
            sp.dma_start(w_sd[I:P, :], sd_in).then_inc(s_ws, 16)
            sp.dma_start(w_gu[:, :, :, :], gu_in).then_inc(s_wgu, 16)
            sp.dma_start(w_down[:, :, :], down_in).then_inc(s_wd, 16)
            sp.dma_start(wq[:, :, :], wq_in).then_inc(s_wa, 16)
            sp.dma_start(wkv[:, :], wkv_in).then_inc(s_wa, 16)
            sp.dma_start(wo[:, :, :], wo_in.rearrange("(j p) c -> p j c", p=P)).then_inc(s_wa, 16)
            for n in range(2):
                ln = 2 * n
                sp.wait_ge(s_xn, 4 * ln + 4)
                sp.dma_start(table_v[:, :, 0:C], xn[:, :, :]).then_inc(s_tab, 16)
                sp.wait_ge(s_wdn, n + 1)
                sp.dma_start(table_v[:, :, C:ROW], wdense[:, :, :]).then_inc(s_tab, 16)
            sp.wait_ge(s_done, 2)
            sp.dma_start(out.rearrange("b (j p) c -> p (b j) c", p=P), x[:, :, :]).then_inc(s_out, 16)
            sp.wait_ge(s_out, 16)

        @block.gpsimd
        def _(pool):
            def gather(n):
                pool.wait_ge(s_tok, n + 1)
                pool.wait_ge(s_tab, 32 * (n + 1))
                for j in range(PAIRS):
                    nc.gpsimd.indirect_dma_start(
                        out=rows[:, j, :], out_offset=None, in_=table,
                        in_offset=bass.IndirectOffsetOnAxis(ap=token_u[:, j:j + 1], axis=0),
                    ).then_inc(s_ga[j // 8], 16)

            def rotate_keys(b):
                for j in range(TPB):
                    wait(pool, s_kvn, b * TPB + (j + 1))
                    wait(pool, s_kr, b * TPB + j)
                    k = kvn[:, j, 0:G * D].rearrange("p (g a r) -> p g a r", g=G, a=2)
                    r3 = [P, G, 32]
                    for a in range(2):
                        nc.gpsimd.tensor_tensor(kt1[:, :, a, :], k[:, :, a, :],
                                                cos_k[:, j, :].unsqueeze(1).to_broadcast(r3), ALU.mult)
                        part = nc.gpsimd.tensor_tensor(kt2[:, :, a, :], k[:, :, 1 - a, :],
                                                       (nsin_k, sin_k)[a][:, j, :].unsqueeze(1).to_broadcast(r3),
                                                       ALU.mult)
                    part.then_inc(s_kpart, 1)
                    pool.wait_ge(s_kpart, b * TPB + (j + 1))
                    wait(pool, s_ktr, (b - 1) * TPB + (j + 1))
                    for a in range(2):
                        last = nc.gpsimd.tensor_tensor(kd[:, j, :, a, :], kt1.rearrange("p g a r -> p g (a r)"),
                                                       kt2.rearrange("p g a r -> p g (a r)"), ALU.add)
                    last.then_inc(s_kr, 1)

            gather(0)
            pool.wait_ge(s_done, 1)
            rotate_keys(0)
            with pool.Fori(1, B) as b:
                rotate_keys(b)
            gather(1)

        @block.tensor
        def _(pe):
            mm = nc.tensor.matmul

            def ln_transposes(ln):
                for g in range(4):
                    pe.wait_ge(s_xn, 4 * ln + g + 1)
                    for t in range(4):
                        last = nc.tensor.transpose(bank[g][:, t * P:(t + 1) * P], xn[:, 4 * g + t, :], ident)
                    last.then_inc(s_xt, 1)

            def ffn(n):
                ln = 2 * n
                ln_transposes(ln)
                if n == 0:
                    pe.wait_ge(s_wr, 16)
                for g in range(4):
                    pe.wait_ge(s_xnT, 4 * ln + g + 1)
                    for t in range(4):
                        i = 4 * g + t
                        last = mm(bank[4 + i // 8][:, (i % 8) * E:(i % 8 + 1) * E], xnT[:, i * P:(i + 1) * P],
                                  w_router[:, :], start=True, stop=True)
                    if g % 2:
                        last.then_inc(s_rt, 1)
                if n == 0:
                    pe.wait_ge(s_ws, 64)
                for r in range(2):
                    for w, o in ((w_sg, 0), (w_su, 2)):
                        for half in range(2):
                            last = mm(bank[r + o][half * I:(half + 1) * I, :], w[:, :],
                                      xnT[:, (2 * r + half) * 512:(2 * r + half + 1) * 512], start=True, stop=True)
                    last.then_inc(s_sgu, 1)
                pe.wait_ge(s_sel, n + 1)
                pe.wait_ge(s_sc, 2 * n + 2)
                for c in range(CH):
                    last = mm(bank[4 + c // 4][:, (c % 4) * P:(c % 4 + 1) * P],
                              sel[:, c * EC:(c + 1) * EC, :].rearrange("p e i -> p (e i)"), tri[:, :],
                              start=True, stop=True)
                last.then_inc(s_inc, 1)
                pe.wait_ge(s_incl, n + 1)
                mm(bank[6][:, 0:CH], before[:, :], incl[:, :, P - 1], start=True, stop=True).then_inc(s_bas, 1)
                pe.wait_ge(s_slt, n + 1)
                for j in range(PAIRS):
                    c, q = j // 4, j % 4
                    pair = slot_tile[:, c, 2 * q:2 * q + 2, :].rearrange("p e s -> p (e s)")
                    last = mm(bank[6][:, 64 + 3 * j:67 + 3 * j], pair, ext[:, c, :], start=True, stop=True)
                last.then_inc(s_pck, 1)
                for c in range(CH):
                    if c >= 3:
                        pe.wait_ge(s_cmp, CH * n + c - 2)
                    for q in range(4):
                        pair = slot_tile[:, c, 2 * q:2 * q + 2, :].rearrange("p e s -> p (e s)")
                        last = mm(bank[(4, 5, 7)[c % 3]][:, q * P:(q + 1) * P], pair, incl[:, c, :],
                                  start=True, stop=True)
                    last.then_inc(s_R, 1)
                for g in range(4):
                    pe.wait_ge(s_sh, 2 * n + 2)
                    for t in range(4):
                        half = g % 2
                        last = mm(bank[g][:, t * P:(t + 1) * P],
                                  hs[half * I:(half + 1) * I, g // 2, t * P:(t + 1) * P],
                                  w_sd[half * I:(half + 1) * I, :], start=True, stop=True)
                    last.then_inc(s_sdn, 1)
                if n == 0:
                    pe.wait_ge(s_wgu, 16)
                    pe.wait_ge(s_wd, 16)

                def gate_up(g):
                    for k in range(8):
                        j = 8 * g + k
                        if k % 4 == 0:
                            pe.wait_ge(s_xgT, CH * n + 2 * g + k // 4 + 1)
                        for o in range(2):
                            for e2 in range(2):
                                e = 2 * j + e2
                                last = mm(bank[2 + 2 * (g % 2) + o][e2 * I:(e2 + 1) * I, k * CAP:(k + 1) * CAP],
                                          w_gu[:, o, e, :], xgT[:, e * CAP:(e + 1) * CAP], start=True, stop=True)
                    last.then_inc(s_gu, 1)

                def down(g):
                    pe.wait_ge(s_h, 4 * n + g // 2 + 1)
                    if g >= 2:
                        pe.wait_ge(s_yw, 8 * n + g - 1)
                    for k in range(4):
                        j = 4 * g + k
                        for e2 in range(2):
                            last = mm(bank[6 + g % 2][e2 * CAP:(e2 + 1) * CAP, k * C:(k + 1) * C],
                                      hT[e2 * I:(e2 + 1) * I, j, :], w_down[e2 * I:(e2 + 1) * I, j, :],
                                      start=True, stop=True)
                    last.then_inc(s_dn, 1)

                pe.wait_ge(s_sx, n + 1)
                pe.wait_ge(s_tok, n + 1)
                for g in range(4):
                    pe.wait_ge(s_ga[g], 128 * (n + 1))
                    for k in range(8):
                        q = 2 * g + k // 4
                        if k % 4 == 0 and q >= 2:
                            pe.wait_ge(s_xgT, CH * n + q - 1)
                        last = nc.tensor.transpose(bank[q % 2][:, (k % 4) * P:(k % 4 + 1) * P],
                                                   rows[:, 8 * g + k, 0:C], ident)
                        if k % 4 == 3:
                            last.then_inc(s_xg, 1)
                    if g >= 2:
                        pe.wait_ge(s_h, 4 * n + g - 1)
                    gate_up(g)
                    if g >= 1:
                        down(2 * g - 2)
                        down(2 * g - 1)
                down(6)
                down(7)
                pe.wait_ge(s_fart, n + 1)
                nc.tensor.transpose(bank[2][0:1, 0:P], far[:, :], ident).then_inc(s_far, 1)
                pe.wait_ge(s_yw, 8 * n + 8)
                pe.wait_ge(s_far_i, n + 1)
                last_tile = pe.value_load(far_i[0:1, 0:1], min_val=0, max_val=(TILES - 1) * P)
                with pe.Fori(0, TILES // 2) as it:
                    with pe.If(it * (2 * P) <= last_tile):
                        for u in range(2):
                            pe.wait_ge(s_oh[n], it * 2 + (u + 1))
                            for j in range(PAIRS):
                                last = mm(bank[u][:, 0:C], onehot[u][:, j, :], yw[:, j, :],
                                          start=(j == 0), stop=(j == PAIRS - 1))
                            last.then_inc(s_cmb[n], 1)

            def kv_proj(b, j):
                wait(pe, s_xb, b + 1)
                if j == 0:
                    wait(pe, s_qr, (b - 1) * HB + 4)
                else:
                    wait(pe, s_kvn, b * TPB + 1)
                mm(bank[2][:, :], xb[:, j * P:(j + 1) * P], wkv[:, :], start=True, stop=True).then_inc(s_kv, 1)

            def k_transposes(b, j):
                wait(pe, s_kr, b * TPB + (j + 1))
                wait(pe, s_qr, b * HB + j)
                for g in range(G):
                    last = nc.tensor.transpose(bank[2 + j][:, g * P:(g + 1) * P],
                                               kd[:, j, g, :, :].rearrange("p a d -> p (a d)"), ident)
                last.then_inc(s_ktr, 1)

            def q_proj(b, p):
                if p in (1, 2):
                    wait(pe, s_kt, b * 2 + 2)
                elif p == 7:
                    wait(pe, s_kvn, (b + 2) * TPB if not isinstance(b, int) or b < B - 1 else 0)
                    wait(pe, s_qr, b * HB + 4)
                else:
                    wait(pe, s_qr, b * HB + {3: 2, 4: 3, 5: 5, 6: 6, 0: -1}[p])
                xs = xnT[:, b * T:(b + 1) * T] if isinstance(b, int) else xnT[:, bass.ds(b * T, T)]
                for k in range(2):
                    last = mm(bank[Q_BANK[p]][:, k * T:(k + 1) * T], wq[:, 2 * p + k, :], xs, start=True, stop=True)
                last.then_inc(s_qp, 1)

            def qk(b, h):
                if h % 2 == 0:
                    wait(pe, s_qr, b * HB + (h // 2 + 1))
                if h == 0:
                    wait(pe, s_kt, b * 2 + 1)
                wait(pe, s_max, b * H + (h - 1))
                g = h // (H // G)
                mm(bank[h % 2][:, 0:P], qT[:, h, 0:P], kT[:, g, 0:P], start=True, stop=True)
                mm(bank[h % 2][:, P:3 * P], qT[:, h, P:T], kT[:, g, :], start=True, stop=True).then_inc(s_qk, 1)

            def p_transposes(b, k):
                wait(pe, s_nrm, b * H + (k + 1))
                wait(pe, s_pt, b * H + (k - 1))
                for t in range(3):
                    last = nc.tensor.transpose(bank[4 + k % 2][:, t * P:(t + 1) * P],
                                               pr[:, k % 4, t * P:(t + 1) * P], ident)
                last.then_inc(s_tr, 1)

            def pv(b, p):
                wait(pe, s_pt, b * H + (2 * p + 2))
                wait(pe, s_y, b * HB + p)
                if p == 0:
                    wait(pe, s_v, b + 1)
                g = 2 * (p % HB) // (H // G)
                for kt in range(TPB):
                    for k in range(2):
                        o = bank[6][k * D:(k + 1) * D, :]
                        q = pT[:, (2 * p + k) % 4, :]
                        last = mm(o[:, 0:T] if kt == 0 else o[:, P:T], v[:, kt, g * D:(g + 1) * D],
                                  q[:, 0:T] if kt == 0 else q[:, T:3 * P], start=(kt == 0), stop=(kt == TPB - 1))
                last.then_inc(s_pv, 1)

            def o_proj(b, p):
                wait(pe, s_y, b * HB + (p + 1))
                if p == 0:
                    wait(pe, s_oadd, b)
                for j in range(TPB):
                    last = mm(bank[7][:, j * C:(j + 1) * C], yT[:, p % HB, j * P:(j + 1) * P], wo[:, p % HB, :],
                              start=(p % HB == 0 and j == 0), stop=(p % HB == HB - 1 and j == TPB - 1),
                              skip_group_check=True)
                last.then_inc(s_o, 1)

            def attention():
                ln_transposes(1)
                pe.wait_ge(s_wa, 48)

                def sequence(b, first=False, last=False, tail=False):
                    for h in range(8 if tail else H):
                        if not tail:
                            if h in Q_AT:
                                q_proj(b, Q_AT[h][0])
                            qk(b, h)
                        if (h >= 3 or not first) and (h < 3 or not tail):
                            p_transposes(b, h - 3)
                        if h % 2 == 0 and (h >= 6 or not first) and (h < 6 or not tail):
                            pv(b, (h - 6) // 2)
                        if h % 2 and (h >= 9 or not first):
                            o_proj(b, (h - 9) // 2)
                        if not last and not tail:
                            if h in KV_AT:
                                kv_proj(b + 1, KV_AT.index(h))
                            if h == Q0_AT:
                                q_proj(b + 1, 0)
                            if h in KT_AT:
                                k_transposes(b + 1, KT_AT.index(h))

                for j in range(TPB):
                    kv_proj(0, j)
                q_proj(0, 0)
                for j in range(TPB):
                    if j == 0:
                        pe.wait_ge(s_kvn, TPB)
                    k_transposes(0, j)
                sequence(0, first=True)
                with pe.Fori(1, B - 1) as b:
                    sequence(b)
                sequence(B - 1, last=True)
                sequence(B, tail=True)

            pe.wait_ge(s_const, 16)
            pe.wait_ge(s_cast, 3)
            ffn(0)
            attention()
            ffn(1)

        @block.scalar
        def _(act):
            def layernorm(ln):
                act.wait_ge(s_var, ln + 1)
                nc.scalar.activation(std[:, :], std[:, :], ACT.Sqrt).then_inc(s_std, 1)
                for g in range(4):
                    act.wait_ge(s_xt, 4 * ln + g + 1)
                    nc.scalar.copy(xnT[:, g * 512:(g + 1) * 512], bank[g][:, :]).then_inc(s_xnT, 1)

            def ffn(n):
                layernorm(2 * n)
                for r in range(2):
                    act.wait_ge(s_rt, 2 * n + r + 1)
                    nc.scalar.activation(scores[:, 8 * r:8 * r + 8, :], bank[4 + r][:, :], ACT.Sigmoid)\
                        .then_inc(s_sc, 1)
                for r in range(2):
                    act.wait_ge(s_sgu, 2 * n + r + 1)
                    nc.scalar.activation(hs[:, r, :], bank[r][:, :], ACT.Silu).then_inc(s_ssilu, 1)
                act.wait_ge(s_inc, n + 1)
                nc.scalar.copy(incl[:, 0:4, :], bank[4][:, :])
                nc.scalar.copy(incl[:, 4:8, :], bank[5][:, :]).then_inc(s_incl, 1)

                def silu(g):
                    act.wait_ge(s_gu, 4 * n + g + 1)
                    if g >= 2:
                        act.wait_ge(s_h, 4 * n + g - 1)
                    nc.scalar.activation(hg[:, g % 2, :], bank[2 + 2 * (g % 2)][:, :], ACT.Silu).then_inc(s_silu, 1)

                for g in range(8):
                    act.wait_ge(s_xg, 8 * n + g + 1)
                    nc.scalar.copy(xgT[:, g * 512:(g + 1) * 512], bank[g % 2][:, :]).then_inc(s_xgT, 1)
                    if g % 2:
                        silu(g // 2)

            def attention():
                layernorm(1)
                act.wait_ge(s_xnT, 8)

                def copy_x(b):
                    wait(act, s_kv, b * TPB)
                    src = xnT[:, b * T:(b + 1) * T] if isinstance(b, int) else xnT[:, bass.ds(b * T, T)]
                    nc.scalar.copy(xb[:, :], src).then_inc(s_xb, 1)

                def copy_kv(b, j):
                    wait(act, s_kv, b * TPB + (j + 1))
                    wait(act, s_kr, (b - 1) * TPB + (j + 1))
                    if j == 0:
                        wait(act, s_v, b)
                    nc.scalar.copy(kvn[:, j, :], bank[2][:, :]).then_inc(s_kvn, 1)

                def copy_k(b, g0, g1):
                    wait(act, s_qk, (b - 1) * H + g1 * (H // G))
                    for j in range(TPB):
                        wait(act, s_ktr, b * TPB + (j + 1))
                        last = nc.scalar.copy(kT[:, g0:g1, j * P:(j + 1) * P],
                                              bank[2 + j][:, g0 * P:g1 * P].rearrange("p (g t) -> p g t", t=P))
                    last.then_inc(s_kt, 1)

                def exps(b, h):
                    wait(act, s_max, b * H + (h + 1))
                    wait(act, s_tr, b * H + (h - 3))
                    k, r = h % 2, h % 4
                    nc.scalar.activation(pr[:, r, 0:P], sm[:, k, 0:P], ACT.Exp, bias=nmax[:, k, 0:1],
                                         scale=-1.0, accum_out=rsum[:, r, 0:1])
                    nc.scalar.activation(pr[:, r, P:3 * P], sm[:, k, P:3 * P], ACT.Exp, bias=nmax[:, k, 1:2],
                                         scale=-1.0, accum_out=rsum[:, r, 1:2]).then_inc(s_exp, 1)

                def copy_p(b, k):
                    wait(act, s_tr, b * H + (k + 1))
                    wait(act, s_pv, b * HB + ((k - 4) // 2 + 1))
                    nc.scalar.copy(pT[:, k % 4, :], bank[4 + k % 2][:, 0:3 * P]).then_inc(s_pt, 1)

                def copy_y(b, p):
                    wait(act, s_pv, b * HB + (p + 1))
                    nc.scalar.copy(yT[:, p % HB, :], bank[6][:, 0:T]).then_inc(s_y, 1)

                def sequence(b, first=False, last=False, tail=False):
                    for h in range(6 if tail else H):
                        if not tail:
                            exps(b, h)
                            if not last and h == H - 1:
                                copy_k(b + 1, G - 1, G)
                        if h % 2 and (h >= 7 or not first):
                            copy_y(b, (h - 7) // 2)
                        if (h >= 3 or not first) and (h < 3 or not tail):
                            copy_p(b, h - 3)
                        if not last and not tail:
                            if h == 3:
                                copy_x(b + 1)
                            if h in KV_AT:
                                copy_kv(b + 1, KV_AT.index(h))
                            if h == KT_AT[1]:
                                copy_k(b + 1, 0, G - 1)

                copy_x(0)
                for j in range(TPB):
                    copy_kv(0, j)
                copy_k(0, 0, G - 1)
                copy_k(0, G - 1, G)
                sequence(0, first=True)
                with act.Fori(1, B - 1) as b:
                    sequence(b)
                sequence(B - 1, last=True)
                sequence(B, tail=True)

            ffn(0)
            attention()
            ffn(1)

        @block.vector
        def _(dve):
            vec = nc.vector
            steps = [0]

            def step(ins):
                steps[0] += 1
                ins.then_inc(s_dve, 1)
                dve.wait_ge(s_dve, steps[0])

            def layernorm(ln):
                for i in range(TILES):
                    last = vec.bn_stats(stats[:, i, :], x[:, i, :])
                step(last)
                for i in range(TILES):
                    last = vec.bn_aggr(meanvar[:, i, :], stats[:, i, :])
                step(last)
                vec.tensor_scalar(std[:, :], meanvar[:, :, 1], EPS, None, ALU.add).then_inc(s_var, 1)
                dve.wait_ge(s_std, ln + 1)
                step(vec.reciprocal(rstd[:, :], std[:, :]))
                if ln == 2:
                    dve.wait_ge(s_tab, 32)
                for i in range(TILES):
                    last = vec.tensor_scalar(xn[:, i, :], x[:, i, :], meanvar[:, i, 0:1], rstd[:, i:i + 1],
                                             ALU.subtract, ALU.mult)
                    if i % 4 == 3:
                        last.then_inc(s_xn, 1)

            def choose(n):
                dve.wait_ge(s_sc, 2 * n + 2)
                sc4 = scores[:, :, :].rearrange("p i (g e) -> p i g e", g=NG)
                step(vec.tensor_reduce(gmax[:, :, 0:NG], sc4, AX, ALU.max))
                for i in range(TILES):
                    last = vec.max(gtop[:, i, :], gmax[:, i, 0:NG])
                step(last)
                step(vec.memset(gtop[:, :, TOPG:8], -1.0))
                for i in range(TILES):
                    last = vec.match_replace(gleft[:, i, :], gtop[:, i, :], gmax[:, i, :], 2.0)
                step(last)
                step(vec.tensor_scalar(gsel[:, :, :], gleft[:, :, 0:NG], 1.5, None, ALU.is_gt))
                step(vec.tensor_tensor(sc4, sc4, gsel[:, :, :].unsqueeze(3).to_broadcast([P, TILES, NG, EG]), ALU.mult))
                for i in range(TILES):
                    last = vec.max(top[:, i, :], scores[:, i, :])
                step(last)
                for i in range(TILES):
                    last = vec.match_replace(left[:, i, :], top[:, i, :], scores[:, i, :], -1.0)
                step(last)
                vec.tensor_scalar(sel[:, :, :].rearrange("p e i -> p i e"), left[:, :, :], 0.0, None, ALU.is_lt)\
                    .then_inc(s_sel, 1)
                step(vec.tensor_reduce(wsum[:, :], top[:, :, :], AX, ALU.add))
                step(vec.tensor_scalar(wsum[:, :], wsum[:, :], 1e-9, None, ALU.max))
                step(vec.reciprocal(wsum[:, :], wsum[:, :]))
                step(vec.tensor_scalar(wsum[:, :], wsum[:, :], 1.25, None, ALU.mult))
                if n == 1:
                    dve.wait_ge(s_tab, 32)
                step(vec.scalar_tensor_tensor(out=wdense[:, :, :], in0=left[:, :, :], scalar=0.0,
                                              in1=scores[:, :, :], op0=ALU.is_lt, op1=ALU.mult))
                vec.tensor_tensor(wdense[:, :, :], wdense[:, :, :], wsum[:, :].unsqueeze(2).to_broadcast([P, TILES, E]),
                                  ALU.mult).then_inc(s_wdn, 1)

            def slots(n):
                dve.wait_ge(s_bas, n + 1)
                vec.tensor_copy(base[:, :], bank[6][:, 0:CH])
                vec.tensor_copy(ext[:, :, 0], bank[6][:, 0:CH])
                step(vec.tensor_tensor(end[:, :], bank[6][:, 0:CH], incl[:, :, P - 1], ALU.add))
                io = iota[:, 0:CAP].unsqueeze(1).to_broadcast([P, CH, CAP])
                vec.tensor_tensor(is_from[:, :, :], io, base[:, :].unsqueeze(2).to_broadcast([P, CH, CAP]), ALU.is_ge)
                step(vec.tensor_tensor(is_to[:, :, :], io, end[:, :].unsqueeze(2).to_broadcast([P, CH, CAP]), ALU.is_lt))
                step(vec.tensor_tensor(is_from[:, :, :], is_from[:, :, :], is_to[:, :, :], ALU.mult))
                vec.tensor_tensor(slot_tile[:, :, :, :],
                                  is_from[:, :, :].unsqueeze(2).to_broadcast([P, CH, EC, CAP]),
                                  own[:, :].unsqueeze(1).unsqueeze(3).to_broadcast([P, CH, EC, CAP]),
                                  ALU.mult).then_inc(s_slt, 1)
                dve.wait_ge(s_pck, n + 1)
                step(vec.tensor_copy(picked[:, :, :], bank[6][:, 64:64 + 3 * PAIRS]))
                step(vec.scalar_tensor_tensor(out=room[:, :], in0=picked[:, :, 0], scalar=-1.0,
                                              in1=slot_no.to_broadcast([P, PAIRS]), op0=ALU.mult, op1=ALU.add))
                for c in range(CH):
                    dve.wait_ge(s_R, CH * n + c + 1)
                    vec.tensor_tensor(is_le[:, 4 * c:4 * c + 4, :],
                                      bank[(4, 5, 7)[c % 3]][:, :].rearrange("p (j t) -> p j t", t=P),
                                      room[:, 4 * c:4 * c + 4].unsqueeze(2).to_broadcast([P, 4, P]),
                                      ALU.is_le).then_inc(s_cmp, 1)
                dve.wait_ge(s_cmp, CH * (n + 1))
                step(vec.tensor_reduce(count[:, :], is_le[:, :, :], AX, ALU.add))
                step(vec.tensor_tensor(token[:, :], count[:, :], picked[:, :, 1], ALU.add))
                vec.tensor_copy(token_u[:, :], token[:, :]).then_inc(s_tok, 1)
                vec.tensor_reduce(far[:, :], picked[:, :, 1], AX, ALU.max).then_inc(s_fart, 1)

            def shared(n):
                for r in range(2):
                    dve.wait_ge(s_ssilu, 2 * n + r + 1)
                    vec.tensor_tensor(hs[:, r, :], hs[:, r, :], bank[2 + r][:, :], ALU.mult).then_inc(s_sh, 1)

            def shared_add(n):
                for g in range(4):
                    dve.wait_ge(s_sdn, 4 * n + g + 1)
                    last = vec.scalar_tensor_tensor(
                        out=x[:, 4 * g:4 * g + 4, :], in0=bank[g][:, :].rearrange("p (i c) -> p i c", c=C), scalar=0.5,
                        in1=x[:, 4 * g:4 * g + 4, :], op0=ALU.mult, op1=ALU.add)
                last.then_inc(s_sx, 1)

            def experts(n):
                for g in range(4):
                    dve.wait_ge(s_ga[g], 128 * (n + 1))
                for e2 in range(2):
                    q = slice(e2 * CAP, (e2 + 1) * CAP)
                    w = bufB[q, C + e2:C + e2 + (PAIRS - 1) * (ROW + 2) + 1:ROW + 2]
                    last = vec.tensor_tensor(wslot[q, :], w, picked[q, :, 2], ALU.mult)
                step(last)
                for g in range(8):
                    if g % 2 == 0:
                        dve.wait_ge(s_silu, 4 * n + g // 2 + 1)
                        dve.wait_ge(s_gu, 4 * n + g // 2 + 1)
                        vec.tensor_tensor(hT[:, 4 * g:4 * g + 8, :], hg[:, (g // 2) % 2, :].rearrange("p (j s) -> p j s", s=CAP),
                                          bank[3 + 2 * ((g // 2) % 2)][:, :].rearrange("p (j s) -> p j s", s=CAP),
                                          ALU.mult).then_inc(s_h, 1)
                    dve.wait_ge(s_dn, 8 * n + g + 1)
                    vec.tensor_tensor(yw[:, 4 * g:4 * g + 4, :], bank[6 + g % 2][:, :].rearrange("p (j c) -> p j c", c=C),
                                      wslot[:, 4 * g:4 * g + 4].unsqueeze(2).to_broadcast([P, 4, C]),
                                      ALU.mult).then_inc(s_yw, 1)
                dve.wait_ge(s_far, n + 1)
                step(vec.tensor_reduce(far1[:, :], bank[2][0:1, 0:P], AX, ALU.max))
                vec.tensor_copy(far_i[:, :], far1[:, :]).then_inc(s_far_i, 1)

            def combine(n):
                dve.wait_ge(s_far_i, n + 1)
                last_tile = dve.value_load(far_i[0:1, 0:1], min_val=0, max_val=(TILES - 1) * P)
                with dve.Fori(0, TILES // 2) as it:
                    with dve.If(it * (2 * P) <= last_tile):
                        for u in range(2):
                            dve.wait_ge(s_rel[n], it * 2 + u)
                            dve.wait_ge(s_cmb[n], it * 2)
                            vec.tensor_tensor(onehot[u], iota.unsqueeze(1).to_broadcast([P, PAIRS, P]),
                                              token[:, :].unsqueeze(2).to_broadcast([P, PAIRS, P]),
                                              ALU.is_equal).then_inc(s_oh[n], 1)
                            dve.wait_ge(s_oh[n], it * 2 + (u + 1))
                            vec.tensor_scalar(token[:, :], token[:, :], -float(P), None, ALU.add).then_inc(s_rel[n], 1)
                        for u in range(2):
                            dve.wait_ge(s_cmb[n], it * 2 + (u + 1))
                            vec.tensor_tensor(x[:, bass.ds(it * 2 + u, 1), :], x[:, bass.ds(it * 2 + u, 1), :],
                                              bank[u][:, 0:C].unsqueeze(1), ALU.add)
                step(vec.memset(far1[:, :], 0.0))
                vec.memset(far1[:, :], 0.0).then_inc(s_done, 1)

            def ffn(n):
                layernorm(2 * n)
                choose(n)
                shared(n)
                slots(n)
                shared_add(n)
                experts(n)
                combine(n)

            def attention():
                layernorm(1)

                def q_rope(b, p):
                    wait(dve, s_qp, b * HB + (p + 1))
                    vec.tensor_tensor(qT[:, 2 * p:2 * p + 2, :], bank[Q_BANK[p]][:, :].rearrange("p (h t) -> p h t", t=T),
                                      rope_q.unsqueeze(1).to_broadcast([P, 2, T]), ALU.mult).then_inc(s_qr, 1)

                def normalise(b, k):
                    r = k % 4
                    wait(dve, s_exp, b * H + (k + 1))
                    vec.reciprocal(rinv[:, r, :], rsum[:, r, :]).then_inc(s_rinv, 1)
                    dve.wait_ge(s_rinv, b * H + (k + 1))
                    vec.tensor_scalar(pr[:, r, 0:P], pr[:, r, 0:P], rinv[:, r, 0:1], None, ALU.mult)
                    vec.tensor_scalar(pr[:, r, P:3 * P], pr[:, r, P:3 * P], rinv[:, r, 1:2], None, ALU.mult)\
                        .then_inc(s_nrm, 1)

                def row_max(b, h):
                    k = h % 2
                    vec.tensor_tensor_reduce(out=sm[:, k, 0:P], in0=bank[k][:, 0:P], in1=causal[:, P:2 * P],
                                             scale=-0.125, scalar=3e38, op0=ALU.add, op1=ALU.min,
                                             accum_out=nmax[:, k, 0:1])
                    vec.tensor_tensor_reduce(out=sm[:, k, P:3 * P], in0=bank[k][:, P:3 * P], in1=causal,
                                             scale=-0.125, scalar=3e38, op0=ALU.add, op1=ALU.min,
                                             accum_out=nmax[:, k, 1:2]).then_inc(s_max, 1)

                def add_o(b):
                    wait(dve, s_o, (b + 1) * HB)
                    xs = x[:, b * TPB:(b + 1) * TPB, :] if isinstance(b, int) else x[:, bass.ds(b * TPB, TPB), :]
                    vec.tensor_tensor(xs, xs, bank[7][:, 0:TPB * C].rearrange("p (j c) -> p j c", c=C), ALU.add)\
                        .then_inc(s_oadd, 1)

                def sequence(b, first=False, last=False, tail=False):
                    for h in range(2 if tail else H):
                        if not tail:
                            dve.wait_ge(s_qk, b * H + (h + 1))
                        if h >= 2 or not first:
                            normalise(b, h - 2)
                        if not tail:
                            row_max(b, h)
                            if h in Q_AT:
                                q_rope(b, Q_AT[h][0])
                            if h == 5:
                                wait(dve, s_pv, b * HB)
                                dve.wait_ge(s_kvn, b * TPB + TPB)
                                vec.tensor_copy(v, kvn[:, :, G * D:2 * G * D]).then_inc(s_v, 1)
                            if not first and h == 8:
                                add_o(b - 1)
                            if not last and h == Q0_AT:
                                q_rope(b + 1, 0)
                    if tail:
                        add_o(B - 1)

                q_rope(0, 0)
                sequence(0, first=True)
                with dve.Fori(1, B - 1) as b:
                    sequence(b)
                sequence(B - 1, last=True)
                sequence(B, tail=True)

            dve.wait_ge(s_const, 16)
            vec.tensor_copy(tri[:, :], tri_f).then_inc(s_cast, 1)
            vec.tensor_copy(before[:, :], before_f).then_inc(s_cast, 1)
            vec.tensor_copy(own[:, :], own_f).then_inc(s_cast, 1)
            vec.tensor_copy(ext[:, :, 1], tile_start.to_broadcast([P, CH]))
            vec.tensor_copy(ext[:, :, 2], ones_col.to_broadcast([P, CH]))
            step(vec.memset(gmax[:, :, NG:], -1.0))
            dve.wait_ge(s_x, 16)
            ffn(0)
            dve.wait_ge(s_done, 1)
            attention()
            dve.wait_ge(s_oadd, B)
            ffn(1)


def shape_constants(np):
    P, T, TILES, EC = 128, 256, 16, 8
    p = np.arange(P)[:, None]
    q = np.arange(P)[None, :]
    inv_freq = (1.0 / np.float32(10000.0) ** (np.arange(0, 64, 2, dtype=np.float32) / np.float32(64))).astype(np.float32)
    angle = (np.arange(T, dtype=np.float32)[:, None] * inv_freq[None, :]).astype(np.float32)
    cos, sin = np.cos(angle), np.sin(angle)
    ck = cos.reshape(2, P, 32).transpose(1, 0, 2).reshape(P, 64)
    sk = sin.reshape(2, P, 32).transpose(1, 0, 2).reshape(P, 64)
    parts = [
        p == q,
        p <= q,
        (p // TILES == q // TILES) & (p < q),
        p // TILES == np.arange(EC)[None, :],
        p % TILES * P,
        np.ones((P, 1)),
        p % 64,
        np.zeros((P, 1)) + q,
        np.zeros((P, P)), np.where(q <= p, 0.0, -1e30),
        np.concatenate([cos, cos, -sin, sin], axis=1).T,
        ck, sk, -sk,
    ]
    return np.ascontiguousarray(np.concatenate([a.astype(np.float32) for a in parts], axis=1))


def kernel(**inputs):
    import numpy as np
    import concourse.bacc as bacc
    from concourse.bass_utils import run_bass_kernel_spmd

    a = {n[3:]: np.asarray(v) for n, v in inputs.items()}
    wq = a["attn_Wq"].reshape(128, 16, 32, 2)
    even, odd = wq[..., 0], wq[..., 1]
    wk = a["attn_Wk"].reshape(128, 4, 32, 2)
    arrays = {
        "x": a["attn_x"],
        "wq": np.concatenate([even, odd, odd, even], axis=2),
        "wkv": np.concatenate([wk.transpose(0, 1, 3, 2).reshape(128, 256), a["attn_Wv"]], axis=1),
        "wo": a["attn_Wo"],
        "router": a["ffn_router_w"],
        "gate_up": np.stack([a["ffn_gate_w"].transpose(1, 0, 2), a["ffn_up_w"].transpose(1, 0, 2)], axis=1),
        "down": a["ffn_down_w"].reshape(32, 128, 128).transpose(1, 0, 2),
        "shared_gate": a["ffn_shared_gate_w"],
        "shared_up": a["ffn_shared_up_w"],
        "shared_down": a["ffn_shared_down_w"],
        "shape_constants": shape_constants(np),
    }
    arrays = {n: np.ascontiguousarray(v) for n, v in arrays.items()}
    nc = bacc.Bacc("TRN2", target_bir_lowering=False, num_devices=1)
    args = [nc.dram_tensor(f"{n}_dram", v.shape, mybir.dt.from_np(v.dtype), kind="ExternalInput").ap() for n, v in arrays.items()]
    args.append(nc.dram_tensor("result", (8, 256, 128), mybir.dt.float32, kind="ExternalOutput").ap())
    macaron_block(nc, *args)
    r = run_bass_kernel_spmd(nc, [{f"{n}_dram": v for n, v in arrays.items()}], core_ids=[0])
    return r.results[0]["result"]
```

```python
import concourse.bass as bass
from concourse import mybir
from contextlib import ExitStack


def macaron_block(nc, x_in, wq_in, wkv_in, wo_in, router_in, gu_in, down_in, sg_in, su_in, sd_in, const_in, out):
    f32 = mybir.dt.float32
    bf16 = mybir.dt.bfloat16
    u32 = mybir.dt.uint32
    i32 = mybir.dt.int32
    ALU = mybir.AluOpType
    ACT = mybir.ActivationFunctionType
    AX = mybir.AxisListType.X

    P = 128
    B, T, C = x_in.shape
    TILES = B * T // P
    TPB = T // P
    H, G, D = 16, 4, 64
    E, I, K, CAP = 64, 64, 8, 64
    NG, TOPG = 8, 4
    EG = E // NG
    PAIRS = E // 2
    CH = E * TILES // P
    EC = P // TILES
    ROW = C + E
    EPS, NEG = 1e-5, -1e30

    ctx = ExitStack()
    with ctx:
        def sb(name, shape, dt=f32):
            return ctx.enter_context(nc.sbuf_tensor(name, shape, dt))

        def sem(name):
            return ctx.enter_context(nc.semaphore(name))

        NCONST = const_in.shape[1]
        const = sb("const", [P, NCONST])
        at = [0]

        def piece(n):
            at[0] += n
            return const[:, at[0] - n:at[0]]

        ident = piece(P)
        tri_f, before_f, own_f = piece(P), piece(P), piece(EC)
        tile_start, ones_col, slot_half = piece(1), piece(1), piece(1)
        iota = piece(P)
        causal = piece(2 * P)
        cos_q, sin_q = piece(T), piece(T)
        cos_k = piece(TPB * 32).rearrange("p (j r) -> p j r", j=TPB)
        sin_k = piece(TPB * 32).rearrange("p (j r) -> p j r", j=TPB)
        nsin_k = piece(TPB * 32).rearrange("p (j r) -> p j r", j=TPB)
        assert at[0] == NCONST
        tri = sb("tri", [P, P], bf16)
        before = sb("before", [P, P], bf16)
        own = sb("own", [P, EC], bf16)
        ext = sb("ext", [P, CH, 3], bf16)
        iota_b = sb("iota_b", [P, P], bf16)

        wq = sb("wq", [P, H, D])
        wkv = sb("wkv", [P, 2 * G * D])
        wo = sb("wo", [P, H * D // P, C])
        w_router = sb("w_router", [P, E])
        w_gu = sb("w_gu", [P, E, 2 * I])
        w_down = sb("w_down", [P, PAIRS, C])
        w_sg = sb("w_sg", [P, I])
        w_su = sb("w_su", [P, I])
        w_sd = sb("w_sd", [P, C])

        x = sb("x", [P, TILES, C])
        xn = sb("xn", [P, TILES, C])
        xnT = sb("xnT", [P, TILES * P])
        stats = sb("stats", [P, TILES, 6])
        meanvar = sb("meanvar", [P, TILES, 2])
        std = sb("std", [P, TILES])
        rstd = sb("rstd", [P, TILES])
        bufA = sb("bufA", [P, PAIRS * P])
        bufB = sb("bufB", [P, PAIRS * ROW])
        xgT = bufA[:, :]
        rows = bufB[:, :].rearrange("p (j c) -> p j c", c=ROW)
        assert ROW * 2 == 3 * C
        yw = bufB[:, :].bitcast(bf16).rearrange("p (j k c) -> p j k c", k=3, c=C)
        onehot = bufA[:, :].bitcast(bf16).rearrange("p (u j t) -> p u j t", u=2, t=P)
        qT = bufA[:, 0:H * T].rearrange("p (h t) -> p h t", t=T)

        scores = sb("scores", [P, TILES, E])
        gmax = sb("gmax", [P, TILES, NG + TOPG])
        gtop = sb("gtop", [P, TILES, 8])
        gleft = sb("gleft", [P, TILES, NG + TOPG])
        gsel = sb("gsel", [P, TILES, NG])
        top = sb("top", [P, TILES, K])
        left = sb("left", [P, TILES, E])
        sel = sb("sel", [P, E, TILES], bf16)
        wsum = sb("wsum", [P, TILES])
        wdense = sb("wdense", [P, TILES, E])
        incl = sb("incl", [P, CH, P], bf16)
        base = sb("base", [P, CH])
        end = sb("end", [P, CH])
        is_from = sb("is_from", [P, CH, CAP], bf16)
        is_to = sb("is_to", [P, CH, CAP], bf16)
        slot_tile = sb("slot_tile", [P, CH, EC, CAP], bf16)
        picked = sb("picked", [P, PAIRS, 3])
        room = sb("room", [P, PAIRS])
        sign = sb("sign", [P, PAIRS, P], bf16)
        count = sb("count", [P, PAIRS])
        token = sb("token", [P, PAIRS])
        token_rel = sb("token_rel", [P, TILES + 2, PAIRS], bf16)
        token_u = sb("token_u", [P, PAIRS], u32)
        wslot = sb("wslot", [P, PAIRS])
        hs = sb("hs", [P, 2, 512])
        hg = sb("hg", [P, 2, 4 * I])
        hidden = sb("hidden", [P, 2, 4, P])
        hT = sb("hT", [P, 2, 4 * P])
        bufC = sb("bufC", [P, PAIRS * C])
        y_all = bufC[:, 0:2 * 4 * C].rearrange("p (k n) -> p k n", k=2)
        y_left = bufC[:, 2 * 4 * C:4 * 4 * C].rearrange("p (k n) -> p k n", k=2)
        far = sb("far", [P, 1])
        far1 = sb("far1", [1, 1])
        far_i = sb("far_i", [1, 1], i32)
        y_sum = sb("y_sum", [P, 2, C])

        xb = sb("xb", [P, T])
        q_raw = sb("q_raw", [P, H // G // 2, T])
        kvn = hT[:, :, :]
        assert 2 * G * D == 4 * P and TPB == 2
        cut = [0]

        def attn(n):
            cut[0] += n
            return bufB[:, cut[0] - n:cut[0]]

        yT = attn(H // 2 * T).rearrange("p (j t) -> p j t", t=T)
        pT = attn(4 * 3 * P).rearrange("p (k t) -> p k t", t=3 * P)
        sm = attn(2 * 3 * P).rearrange("p (k t) -> p k t", t=3 * P)
        kd = attn(TPB * G * 2 * D).rearrange("p (j g a d) -> p j g a d", j=TPB, g=G, a=2)
        n0, n1, n2 = G * T, G * T + TPB * G * D, G * T + TPB * G * D + G * D
        kT = bufC[:, 0:n0].rearrange("p (g t) -> p g t", g=G)
        v = bufC[:, n0:n1].rearrange("p (j n) -> p j n", j=TPB)
        kt1 = bufC[:, n1:n2].rearrange("p (g a r) -> p g a r", g=G, a=2)
        n3 = n2 + G * D
        kt2 = bufC[:, n2:n3].rearrange("p (g a r) -> p g a r", g=G, a=2)
        pr = bufC[:, n3:n3 + 4 * 3 * P].rearrange("p (k t) -> p k t", t=3 * P)
        nmax = sb("nmax", [P, 2, 2])
        rsum = sb("rsum", [P, 4, 2])
        rinv = sb("rinv", [P, 4, 2])

        bank = [ctx.enter_context(nc.psum_tensor(f"bank{i}", [P, 512], f32)) for i in range(8)]
        table = nc.dram_tensor("gather_table", [TILES * P, ROW], f32, kind="Internal").ap()
        table_v = table.rearrange("(i p) c -> p i c", p=P)

        s_const, s_wr, s_ws, s_wgu, s_wd, s_wa = [sem(n) for n in (
            "const_in", "router_in", "shared_in", "gate_up_in", "down_in", "attn_w_in")]
        s_x = [sem(f"x_in{g}") for g in range(4)]
        s_dve = sem("dve_step")
        s_cast = sem("const_cast")
        s_early = sem("early_statistics")
        s_var = sem("variance")
        s_std = sem("std")
        s_xn = sem("xn_group")
        s_xt = sem("xnT_psum")
        s_xnT = sem("xnT")
        s_rt = sem("logits")
        s_sc = sem("scores")
        s_sel = sem("selected")
        s_wdn = sem("dense_weights")
        s_tab = sem("table_stored")
        s_inc = sem("prefix_psum")
        s_incl = sem("prefix")
        s_bas = sem("base_psum")
        s_slt = sem("slot_tile")
        s_pck = sem("picked_psum")
        s_R = sem("prefix_of_slot")
        s_room = sem("room")
        s_picked = sem("picked")
        s_trel = sem("token_rel")
        s_cmp = sem("signs_summed")
        s_tok = sem("token_of_slot")
        s_ga = [sem(f"gathered{i}") for i in range(CH)]
        s_xg = sem("xgT_psum")
        s_xgT = sem("xgT")
        s_gu = sem("gate_up_psum")
        s_silu = sem("silu")
        s_h = sem("hidden")
        s_htp = sem("hT_psum")
        s_hT = sem("hT")
        s_dn = sem("down_psum")
        s_wsl = sem("slot_weights")
        s_yall = sem("weighted_out")
        s_hi = sem("high_part")
        s_left = sem("left_by_high")
        s_mid = sem("middle_part")
        s_yw = sem("low_part")
        s_sgu = sem("shared_gu_psum")
        s_ssilu = sem("shared_silu")
        s_sh = sem("shared_hidden")
        s_sdn = sem("shared_down_psum")
        s_sx = sem("shared_added")
        s_far = sem("last_tile_psum")
        s_fart = sem("last_tile_partial")
        s_far_i = sem("last_tile")
        s_oh = [sem(f"onehot_ffn{n}") for n in range(2)]
        s_cmb = [sem(f"combined_ffn{n}") for n in range(2)]
        s_sum = [sem(f"parts_summed_ffn{n}") for n in range(2)]
        s_add = [sem(f"added_ffn{n}") for n in range(2)]
        s_done = sem("ffn_done")

        s_xb = sem("xb")
        s_kv = sem("kv_psum")
        s_kvn = sem("kv_next")
        s_v = sem("v")
        s_kpart = sem("k_rope_parts")
        s_rinv = sem("row_sum_inverse")
        s_kr = sem("k_rope")
        s_ktr = sem("kT_psum")
        s_kt = sem("kT")
        s_qp = sem("q_psum")
        s_qc = sem("q_copied")
        s_qrot = sem("q_rope_dve")
        s_qsin = sem("q_sin")
        s_qk = sem("scores_psum")
        s_max = sem("row_max")
        s_exp = sem("exp")
        s_nrm = sem("normalised")
        s_tr = sem("pT_psum")
        s_pt = sem("pT")
        s_pv = sem("y_psum")
        s_y = sem("yT")
        s_o = sem("o_psum")
        s_oadd = sem("attn_added")
        s_out = sem("out_stored")

        def wait(eng, s, count):
            if not isinstance(count, int) or count > 0:
                eng.wait_ge(s, count)

        SHARED_BANK = (0, 2, 1, 3)
        LN_TILES = ([range(TILES)], [range(4 * g, 4 * g + 4) for g in range(4)], [range(12), range(12, TILES)])
        PARTS_BEFORE = (0, 1, 5)
        LN_BANK = (0, 4, 0)
        HB = H // 2

        def heads(g, e2):
            return qT[:, 4 * g:4 * g + 4, :].rearrange("p (k e) t -> p e k t", e=2)[:, e2]

        Q_AT = {1: 1, 4: 2, 8: 3}
        ROPE_AT = {2: (1, (0, 1, 2)), 5: (2, (0,)), 6: (2, (1, 2)), 9: (3, (0, 1)), 10: (3, (2,))}
        ROPE0_AT = {13: (0,), 14: (1, 2)}
        KV_AT, Q0_AT, KT_AT = (6, 8), 12, (13, 14)
        Q_BANK = (3, 2, 3, 3)

        block = ctx.enter_context(nc.Block())

        @block.sync
        def _(sp):
            x_tiles = x_in.rearrange("b (j p) c -> p (b j) c", p=P)
            for g in range(4):
                sp.dma_start(x[:, 4 * g:4 * g + 4, :], x_tiles[:, 4 * g:4 * g + 4, :]).then_inc(s_x[g], 16)
            sp.dma_start(w_router[:, :], router_in).then_inc(s_wr, 16)
            sp.dma_start(w_sg[:, :], sg_in).then_inc(s_ws, 16)
            sp.dma_start(w_su[:, :], su_in).then_inc(s_ws, 16)
            sp.dma_start(w_sd[0:I, :], sd_in).then_inc(s_ws, 16)
            sp.dma_start(w_sd[I:P, :], sd_in).then_inc(s_ws, 16)
            sp.dma_start(w_gu[:, :, :], gu_in).then_inc(s_wgu, 16)
            sp.dma_start(w_down[:, :, :], down_in).then_inc(s_wd, 16)
            sp.dma_start(wq[:, :, :], wq_in).then_inc(s_wa, 16)
            sp.dma_start(wkv[:, :], wkv_in).then_inc(s_wa, 16)
            sp.dma_start(wo[:, :, :], wo_in.rearrange("(j p) c -> p j c", p=P)).then_inc(s_wa, 16)
            for n in range(2):
                ln = 2 * n
                sp.wait_ge(s_xn, 4 * ln + 4)
                sp.dma_start(table_v[:, :, 0:C], xn[:, :, :]).then_inc(s_tab, 16)
                sp.wait_ge(s_wdn, n + 1)
                sp.dma_start(table_v[:, :, C:ROW], wdense[:, :, :]).then_inc(s_tab, 16)
            sp.wait_ge(s_done, 2)
            sp.dma_start(out.rearrange("b (j p) c -> p (b j) c", p=P), x[:, :, :]).then_inc(s_out, 16)
            sp.wait_ge(s_out, 16)

        @block.gpsimd
        def _(pool):
            def gather(n):
                pool.wait_ge(s_tab, 32 * (n + 1))
                for j in range(PAIRS):
                    if j % 4 == 0:
                        pool.wait_ge(s_tok, CH * n + j // 4 + 1)
                    nc.gpsimd.indirect_dma_start(
                        out=rows[:, j, :], out_offset=None, in_=table,
                        in_offset=bass.IndirectOffsetOnAxis(ap=token_u[:, j:j + 1], axis=0),
                    ).then_inc(s_ga[j // 4], 16)

            def rotate_keys(b, j):
                wait(pool, s_kvn, b * TPB + (j + 1))
                wait(pool, s_kr, b * TPB + j)
                k = kvn[:, j, 0:G * D].rearrange("p (g a r) -> p g a r", g=G, a=2)
                r3 = [P, G, 32]
                for a in range(2):
                    nc.gpsimd.tensor_tensor(kt1[:, :, a, :], k[:, :, a, :],
                                            cos_k[:, j, :].unsqueeze(1).to_broadcast(r3), ALU.mult)
                    part = nc.gpsimd.tensor_tensor(kt2[:, :, a, :], k[:, :, 1 - a, :],
                                                   (nsin_k, sin_k)[a][:, j, :].unsqueeze(1).to_broadcast(r3), ALU.mult)
                part.then_inc(s_kpart, 1)
                pool.wait_ge(s_kpart, b * TPB + (j + 1))
                wait(pool, s_ktr, (b - 1) * TPB + (j + 1))
                nc.gpsimd.tensor_tensor(kd[:, j, :, 0, :], kt1.rearrange("p g a r -> p g (a r)"),
                                        kt2.rearrange("p g a r -> p g (a r)"), ALU.add)
                for a in range(2):
                    last = nc.gpsimd.tensor_tensor(kd[:, j, :, 1, (1 - a) * 32:(2 - a) * 32], kt1[:, :, a, :],
                                                   kt2[:, :, a, :], ALU.add)
                last.then_inc(s_kr, 1)

            def sines(b, g):
                wait(pool, s_qc, b * G + (g + 1))
                wait(pool, s_kr, (b + 1) * TPB + (1 if g == 3 and not isinstance(b, int) else 0))
                nc.gpsimd.tensor_tensor(heads(g, 1)[D:P], q_raw[D:P, :, :],
                                        sin_q[D:P].unsqueeze(1).to_broadcast([D, 2, T]), ALU.mult).then_inc(s_qsin, 1)
                wait(pool, s_qsin, b * G + (g + 1))

            gather(0)
            pool.wait_ge(s_done, 1)
            rotate_keys(0, 0)
            rotate_keys(0, 1)
            sines(0, 0)
            with pool.Fori(0, B - 1) as b:
                sines(b, 1)
                sines(b, 2)
                rotate_keys(b + 1, 0)
                sines(b, 3)
                rotate_keys(b + 1, 1)
                sines(b + 1, 0)
            for g in range(1, G):
                sines(B - 1, g)
            gather(1)

        @block.tensor
        def _(pe):
            mm = nc.tensor.matmul

            def ln_transposes(ln, g):
                pe.wait_ge(s_xn, 4 * ln + g + 1)
                for t in range(4):
                    last = nc.tensor.transpose(bank[LN_BANK[ln] + g][:, t * P:(t + 1) * P], xn[:, 4 * g + t, :], ident)
                last.then_inc(s_xt, 1)

            def ffn(n):
                ln = 2 * n

                def router(g):
                    pe.wait_ge(s_xnT, 4 * ln + g + 1)
                    for i in range(4 * g, 4 * g + 4):
                        last = mm(bank[4 + i // 8][:, (i % 8) * E:(i % 8 + 1) * E], xnT[:, i * P:(i + 1) * P],
                                  w_router[:, :], start=True, stop=True)
                    if g % 2:
                        last.then_inc(s_rt, 1)

                if n == 0:
                    pe.wait_ge(s_wr, 16)
                if n == 0:
                    ln_transposes(ln, 0)
                    for g in range(4):
                        if g < 3:
                            ln_transposes(ln, g + 1)
                        router(g)
                else:
                    for g in range(3):
                        router(g)
                    ln_transposes(ln, 3)
                    router(3)
                if n == 0:
                    pe.wait_ge(s_ws, 64)
                for r in range(2):
                    for w, o in ((w_sg, 0), (w_su, 2)):
                        for half in range(2):
                            last = mm(bank[r + o][half * I:(half + 1) * I, :], w[:, :],
                                      xnT[:, (2 * r + half) * 512:(2 * r + half + 1) * 512], start=True, stop=True)
                    last.then_inc(s_sgu, 1)
                def shared_down(g):
                    half = g % 2
                    pe.wait_ge(s_sh, 2 * n + g // 2 + 1)
                    for t in range(4):
                        last = mm(bank[SHARED_BANK[g]][:, t * P:(t + 1) * P],
                                  hs[half * I:(half + 1) * I, g // 2, t * P:(t + 1) * P],
                                  w_sd[half * I:(half + 1) * I, :], start=True, stop=True)
                    last.then_inc(s_sdn, 1)

                shared_down(0)
                shared_down(1)
                if n == 0:
                    pe.wait_ge(s_cast, 3)
                pe.wait_ge(s_sel, 2 * n + 2)
                pe.wait_ge(s_sc, 2 * n + 2)
                for c in range(CH):
                    last = mm(bank[4 + c // 4][:, (c % 4) * P:(c % 4 + 1) * P],
                              sel[:, c * EC:(c + 1) * EC, :].rearrange("p e i -> p (e i)"), tri[:, :],
                              start=True, stop=True)
                last.then_inc(s_inc, 1)
                pe.wait_ge(s_incl, n + 1)
                mm(bank[6][:, 0:CH], before[:, :], incl[:, :, P - 1], start=True, stop=True).then_inc(s_bas, 1)
                shared_down(2)
                shared_down(3)
                for c in range(CH):
                    pe.wait_ge(s_slt, CH * n + c + 1)
                    if c >= 2:
                        pe.wait_ge(s_picked, CH * n + c - 1)
                        pe.wait_ge(s_cmp, CH * n + c - 1)
                    pairs = [slot_tile[:, c, 2 * q:2 * q + 2, :].rearrange("p e s -> p (e s)") for q in range(4)]
                    for q in range(4):
                        last = mm(bank[6 + c % 2][:, 64 + 3 * (4 * c + q):67 + 3 * (4 * c + q)], pairs[q], ext[:, c, :],
                                  start=True, stop=True)
                    last.then_inc(s_pck, 1)
                    for q in range(4):
                        last = mm(bank[4 + c % 2][:, q * P:(q + 1) * P], pairs[q], incl[:, c, :],
                                  start=True, stop=True)
                    last.then_inc(s_R, 1)
                if n == 0:
                    pe.wait_ge(s_wgu, 16)
                    pe.wait_ge(s_wd, 16)

                def gather_transposes(c):
                    pe.wait_ge(s_ga[c], 64 * (n + 1))
                    if c < 2:
                        pe.wait_ge(s_sx, 4 * n + (1, 3)[c])
                    if c >= 2:
                        pe.wait_ge(s_xgT, CH * n + c - 1)
                    for k in range(4):
                        last = nc.tensor.transpose(bank[c % 2][:, k * P:(k + 1) * P], rows[:, 4 * c + k, 0:C], ident)
                    last.then_inc(s_xg, 1)

                def gate_up(c):
                    pe.wait_ge(s_xgT, CH * n + c + 1)
                    if c < 2:
                        pe.wait_ge(s_sx, 4 * n + (2, 4)[c])
                    if c >= 2:
                        pe.wait_ge(s_h, CH * n + c - 1)
                    for k in range(4):
                        for e2 in range(2):
                            e = 2 * (4 * c + k) + e2
                            last = mm(bank[2 + c % 2][e2 * CAP:(e2 + 1) * CAP, k * P:(k + 1) * P],
                                      xgT[:, e * CAP:(e + 1) * CAP], w_gu[:, e, :], start=True, stop=True)
                    last.then_inc(s_gu, 1)

                def hidden_transposes(c):
                    pe.wait_ge(s_h, CH * n + c + 1)
                    if c == 0:
                        pe.wait_ge(s_cmp, CH * (n + 1))
                    if c >= 2:
                        pe.wait_ge(s_hT, CH * n + c - 1)
                    for k in range(4):
                        last = nc.tensor.transpose(bank[4 + c % 2][:, k * P:(k + 1) * P], hidden[:, c % 2, k, :], ident)
                    last.then_inc(s_htp, 1)

                def down(c):
                    pe.wait_ge(s_hT, CH * n + c + 1)
                    if c == 0:
                        pe.wait_ge(s_picked, CH * (n + 1))
                    if c >= 2:
                        pe.wait_ge(s_yall, CH * n + c - 1)
                    for k in range(4):
                        last = mm(bank[6 + c % 2][:, k * C:(k + 1) * C], hT[:, c % 2, k * P:(k + 1) * P],
                                  w_down[:, 4 * c + k, :], start=True, stop=True)
                    last.then_inc(s_dn, 1)

                gather_transposes(0)
                for c in range(CH):
                    if c == CH - 1:
                        pe.wait_ge(s_fart, n + 1)
                        nc.tensor.transpose(bank[0][0:1, 0:P], far[:, :], ident).then_inc(s_far, 1)
                    gate_up(c)
                    if c >= 1:
                        down(c - 1)
                    if c + 1 < CH:
                        gather_transposes(c + 1)
                    hidden_transposes(c)
                down(CH - 1)
                pe.wait_ge(s_yw, CH * (n + 1) - 3)
                pe.wait_ge(s_far_i, n + 1)
                last_tile = pe.value_load(far_i[0:1, 0:1], min_val=0, max_val=TILES * P)
                with pe.Fori(0, TILES // 2) as it:
                    with pe.If(it * (2 * P) <= last_tile):
                        for u in range(2):
                            pe.wait_ge(s_oh[n], it * 2 + (u + 1))
                            pe.wait_ge(s_sum[n], it * 2 + (u + 1))
                            for j in range(PAIRS):
                                if j % 4 == 0 and j >= PAIRS - 12:
                                    pe.wait_ge(s_yw, CH * n + j // 4 + 1)
                                last = mm(bank[u][:, 0:3 * C], onehot[:, u, j, :], yw[:, j, :, :],
                                          start=(j == 0), stop=(j == PAIRS - 1))
                            last.then_inc(s_cmb[n], 1)

            def kv_proj(b, j):
                wait(pe, s_xb, b + 1)
                if j == 0:
                    wait(pe, s_qc, (b - 1) * G + 2)
                else:
                    wait(pe, s_kvn, b * TPB + 1)
                mm(bank[2][:, :], xb[:, j * P:(j + 1) * P], wkv[:, :], start=True, stop=True).then_inc(s_kv, 1)

            def k_transposes(b, j):
                wait(pe, s_kr, b * TPB + (j + 1))
                if j == 1:
                    wait(pe, s_qc, b * G + 1)
                for g in range(G):
                    last = nc.tensor.transpose(bank[2 + j][:, g * P:(g + 1) * P],
                                               kd[:, j, g, :, :].rearrange("p a d -> p (a d)"), ident)
                last.then_inc(s_ktr, 1)

            def q_proj(b, g):
                if g == 1:
                    wait(pe, s_kt, b * 2 + 2)
                elif g != 2:
                    wait(pe, s_qc, b * G + g)
                xs = xnT[:, b * T:(b + 1) * T] if isinstance(b, int) else xnT[:, bass.ds(b * T, T)]
                for k in range(2):
                    last = mm(bank[Q_BANK[g]][:, k * T:(k + 1) * T],
                              wq[:, 4 * g + 2 * k:4 * g + 2 * k + 2, :].rearrange("p h d -> p (h d)"), xs,
                              start=True, stop=True)
                last.then_inc(s_qp, 1)

            def qk(b, h):
                if h % 4 == 0:
                    wait(pe, s_qrot, 3 * (b * G + (h // 4 + 1)))
                    wait(pe, s_qsin, b * G + (h // 4 + 1))
                if h == 0:
                    wait(pe, s_kt, b * 2 + 1)
                wait(pe, s_max, b * H + (h - 1))
                g = h // (H // G)
                mm(bank[h % 2][:, 0:P], qT[:, h, 0:P], kT[:, g, 0:P], start=True, stop=True)
                mm(bank[h % 2][:, P:3 * P], qT[:, h, P:T], kT[:, g, :], start=True, stop=True).then_inc(s_qk, 1)

            def p_transposes(b, k):
                wait(pe, s_nrm, b * H + (k + 1))
                wait(pe, s_pt, b * H + (k - 1))
                for t in range(3):
                    last = nc.tensor.transpose(bank[4 + k % 2][:, t * P:(t + 1) * P],
                                               pr[:, k % 4, t * P:(t + 1) * P], ident)
                last.then_inc(s_tr, 1)

            def pv(b, p):
                wait(pe, s_pt, b * H + (2 * p + 2))
                wait(pe, s_y, b * HB + p)
                if p == 0:
                    wait(pe, s_v, b + 1)
                g = 2 * (p % HB) // (H // G)
                for kt in range(TPB):
                    for k in range(2):
                        o = bank[6][k * D:(k + 1) * D, :]
                        q = pT[:, (2 * p + k) % 4, :]
                        last = mm(o[:, 0:T] if kt == 0 else o[:, P:T], v[:, kt, g * D:(g + 1) * D],
                                  q[:, 0:T] if kt == 0 else q[:, T:3 * P], start=(kt == 0), stop=(kt == TPB - 1))
                last.then_inc(s_pv, 1)

            def o_proj(b, p):
                wait(pe, s_y, b * HB + (p + 1))
                if p == 0:
                    wait(pe, s_oadd, b)
                for j in range(TPB):
                    last = mm(bank[7][:, j * C:(j + 1) * C], yT[:, p % HB, j * P:(j + 1) * P], wo[:, p % HB, :],
                              start=(p % HB == 0 and j == 0), stop=(p % HB == HB - 1 and j == TPB - 1),
                              skip_group_check=True)
                last.then_inc(s_o, 1)

            def attention():
                pe.wait_ge(s_wa, 48)

                def sequence(b, first=False, last=False, tail=False):
                    for h in range(10 if tail else H):
                        if not tail:
                            qk(b, h)
                            if h in Q_AT:
                                q_proj(b, Q_AT[h])
                        if h % 2 and (h >= 7 or not first) and (h < 7 or not tail):
                            pv(b, (h - 7) // 2)
                        if (h >= 3 or not first) and (h < 3 or not tail):
                            p_transposes(b, h - 3)
                        if h % 2 == 0 and (h >= 10 or not first):
                            o_proj(b, (h - 10) // 2)
                        if tail and h in (5, 6, 8):
                            ln_transposes(2, (5, 6, 8).index(h))
                        if not last and not tail:
                            if h in KV_AT:
                                kv_proj(b + 1, KV_AT.index(h))
                            if h == Q0_AT:
                                q_proj(b + 1, 0)
                            if h in KT_AT:
                                k_transposes(b + 1, KT_AT.index(h))

                ln_transposes(1, 0)
                kv_proj(0, 0)
                q_proj(0, 0)
                kv_proj(0, 1)
                ln_transposes(1, 1)
                ln_transposes(1, 2)
                ln_transposes(1, 3)
                for j in range(TPB):
                    if j == 0:
                        pe.wait_ge(s_kvn, TPB)
                    k_transposes(0, j)
                pe.wait_ge(s_xnT, 8)
                sequence(0, first=True)
                with pe.Fori(1, B - 1) as b:
                    sequence(b)
                sequence(B - 1, last=True)
                sequence(B, tail=True)

            pe.wait_ge(s_const, 16)
            ffn(0)
            attention()
            ffn(1)

        @block.scalar
        def _(act):
            act.dma_start(const[:, :], const_in).then_inc(s_const, 16)

            def root(ln, part):
                tiles = LN_TILES[ln][part]
                q = slice(tiles[0], tiles[-1] + 1)
                act.wait_ge(s_var, PARTS_BEFORE[ln] + part + 1)
                nc.scalar.activation(std[:, q], std[:, q], ACT.Sqrt).then_inc(s_std, 1)

            def copy_xnT(ln, g):
                act.wait_ge(s_xt, 4 * ln + g + 1)
                nc.scalar.copy(xnT[:, g * 512:(g + 1) * 512], bank[LN_BANK[ln] + g][:, :]).then_inc(s_xnT, 1)

            def ffn(n):
                root(2 * n, n)
                for g in range(3 * n, 3):
                    copy_xnT(2 * n, g)
                for r in range(2):
                    if r == 1:
                        copy_xnT(2 * n, 3)
                    act.wait_ge(s_rt, 2 * n + r + 1)
                    nc.scalar.activation(scores[:, 8 * r:8 * r + 8, :], bank[4 + r][:, :], ACT.Sigmoid)\
                        .then_inc(s_sc, 1)
                for r in range(2):
                    act.wait_ge(s_sgu, 2 * n + r + 1)
                    nc.scalar.activation(hs[:, r, :], bank[r][:, :], ACT.Silu).then_inc(s_ssilu, 1)
                act.wait_ge(s_inc, n + 1)
                nc.scalar.copy(incl[:, 0:4, :], bank[4][:, :])
                nc.scalar.copy(incl[:, 4:8, :], bank[5][:, :]).then_inc(s_incl, 1)

                def copy_gathered(c):
                    act.wait_ge(s_xg, CH * n + c + 1)
                    nc.scalar.copy(xgT[:, c * 512:(c + 1) * 512], bank[c % 2][:, :]).then_inc(s_xgT, 1)

                for c in range(CH):
                    if c == CH - 1:
                        copy_gathered(0)
                    act.wait_ge(s_R, CH * n + c + 1)
                    act.wait_ge(s_room, CH * n + c + 1)
                    for q in range(4):
                        j = 4 * c + q
                        last = nc.scalar.activation(sign[:, j, :], bank[4 + c % 2][:, q * P:(q + 1) * P], ACT.Sign,
                                                    bias=room[:, j:j + 1], scale=-1.0, accum_out=count[:, j:j + 1])
                    last.then_inc(s_cmp, 1)

                for c in range(CH + 2):
                    if 1 <= c <= CH:
                        k = c - 1
                        act.wait_ge(s_htp, CH * n + k + 1)
                        if k >= 2:
                            act.wait_ge(s_dn, CH * n + k - 1)
                        nc.scalar.copy(hT[:, k % 2, :], bank[4 + k % 2][:, :]).then_inc(s_hT, 1)
                    if c < CH:
                        act.wait_ge(s_gu, CH * n + c + 1)
                        if c >= 2:
                            act.wait_ge(s_h, CH * n + c - 1)
                        nc.scalar.activation(hg[:, c % 2, :].rearrange("p (j i) -> p j i", i=I),
                                             bank[2 + c % 2][:, :].rearrange("p (j i) -> p j i", i=2 * I)[:, :, 0:I],
                                             ACT.Silu).then_inc(s_silu, 1)
                    if c + 1 < CH:
                        copy_gathered(c + 1)
                    if c >= 2:
                        k = c - 2
                        act.wait_ge(s_left, CH * n + k + 1)
                        nc.scalar.copy(yw[:, 4 * k:4 * k + 4, 1, :], y_left[:, k % 2, :].rearrange("p (j c) -> p j c", c=C))\
                            .then_inc(s_mid, 1)
                    if 1 <= c <= CH:
                        k = c - 1
                        act.wait_ge(s_yall, CH * n + k + 1)
                        nc.scalar.copy(yw[:, 4 * k:4 * k + 4, 0, :], y_all[:, k % 2, :].rearrange("p (j c) -> p j c", c=C))\
                            .then_inc(s_hi, 1)

            def attention():
                def copy_x(b):
                    wait(act, s_kv, b * TPB)
                    src = xnT[:, b * T:(b + 1) * T] if isinstance(b, int) else xnT[:, bass.ds(b * T, T)]
                    nc.scalar.copy(xb[:, :], src).then_inc(s_xb, 1)

                def copy_kv(b, j):
                    wait(act, s_kv, b * TPB + (j + 1))
                    wait(act, s_kr, (b - 1) * TPB + (j + 1))
                    if j == 0:
                        wait(act, s_v, b)
                    nc.scalar.copy(kvn[:, j, :], bank[2][:, :]).then_inc(s_kvn, 1)

                def copy_q(b, g):
                    wait(act, s_qp, b * G + (g + 1))
                    wait(act, s_qrot, 3 * (b * G + g))
                    wait(act, s_qsin, b * G + g)
                    nc.scalar.copy(q_raw.rearrange("p k t -> p (k t)"), bank[Q_BANK[g]][:, :]).then_inc(s_qc, 1)

                def copy_k(b, g0, g1):
                    wait(act, s_qk, (b - 1) * H + g1 * (H // G))
                    for j in range(TPB):
                        wait(act, s_ktr, b * TPB + (j + 1))
                        last = nc.scalar.copy(kT[:, g0:g1, j * P:(j + 1) * P],
                                              bank[2 + j][:, g0 * P:g1 * P].rearrange("p (g t) -> p g t", t=P))
                    last.then_inc(s_kt, 1)

                def exps(b, h):
                    wait(act, s_max, b * H + (h + 1))
                    wait(act, s_tr, b * H + (h - 3))
                    k, r = h % 2, h % 4
                    nc.scalar.activation(pr[:, r, 0:P], sm[:, k, 0:P], ACT.Exp, bias=nmax[:, k, 0:1],
                                         scale=-1.0, accum_out=rsum[:, r, 0:1])
                    nc.scalar.activation(pr[:, r, P:3 * P], sm[:, k, P:3 * P], ACT.Exp, bias=nmax[:, k, 1:2],
                                         scale=-1.0, accum_out=rsum[:, r, 1:2]).then_inc(s_exp, 1)

                def copy_p(b, k):
                    wait(act, s_tr, b * H + (k + 1))
                    wait(act, s_pv, b * HB + ((k - 4) // 2 + 1))
                    nc.scalar.copy(pT[:, k % 4, :], bank[4 + k % 2][:, 0:3 * P]).then_inc(s_pt, 1)

                def copy_y(b, p):
                    wait(act, s_pv, b * HB + (p + 1))
                    nc.scalar.copy(yT[:, p % HB, :], bank[6][:, 0:T]).then_inc(s_y, 1)

                def sequence(b, first=False, last=False, tail=False):
                    for h in range(7 if tail else H):
                        if h % 2 == 0 and (h >= 8 or not first):
                            copy_y(b, (h - 8) // 2)
                        if tail and h == 3:
                            root(2, 0)
                        if (h >= 3 or not first) and (h < 3 or not tail):
                            copy_p(b, h - 3)
                        if not tail:
                            exps(b, h)
                            if not last and h == H - 1:
                                copy_k(b + 1, G - 1, G)
                        if not tail and h in Q_AT:
                            copy_q(b, Q_AT[h])
                        if not last and not tail:
                            if h == Q0_AT:
                                copy_q(b + 1, 0)
                            if h == 3:
                                copy_x(b + 1)
                            if h in KV_AT:
                                copy_kv(b + 1, KV_AT.index(h))
                            if h == KT_AT[1]:
                                copy_k(b + 1, 0, G - 1)

                root(1, 0)
                copy_xnT(1, 0)
                act.wait_ge(s_xnT, 5)
                copy_x(0)
                root(1, 1)
                root(1, 2)
                copy_kv(0, 0)
                copy_kv(0, 1)
                copy_q(0, 0)
                copy_xnT(1, 1)
                root(1, 3)
                copy_xnT(1, 2)
                copy_xnT(1, 3)
                act.wait_ge(s_xnT, 8)
                copy_k(0, 0, G - 1)
                copy_k(0, G - 1, G)
                sequence(0, first=True)
                with act.Fori(1, B - 1) as b:
                    sequence(b)
                sequence(B - 1, last=True)
                sequence(B, tail=True)
                for g in range(3):
                    copy_xnT(2, g)

            ffn(0)
            attention()
            ffn(1)

        @block.vector
        def _(dve):
            vec = nc.vector
            steps = [0]

            def step(ins):
                steps[0] += 1
                ins.then_inc(s_dve, 1)
                dve.wait_ge(s_dve, steps[0])

            def statistics(ln, part):
                tiles = LN_TILES[ln][part]
                for i in tiles:
                    if ln == 0 and i % 4 == 0:
                        dve.wait_ge(s_x[i // 4], 16)
                    last = vec.bn_stats(stats[:, i, :], x[:, i, :])
                step(last)
                for i in tiles:
                    last = vec.bn_aggr(meanvar[:, i, :], stats[:, i, :])
                step(last)
                variance(tiles)

            def variance(tiles):
                q = slice(tiles[0], tiles[-1] + 1)
                vec.tensor_scalar(std[:, q], meanvar[:, q, 1], EPS, None, ALU.add).then_inc(s_var, 1)

            def normalise_tokens(ln, part):
                tiles = LN_TILES[ln][part]
                q = slice(tiles[0], tiles[-1] + 1)
                dve.wait_ge(s_std, PARTS_BEFORE[ln] + part + 1)
                step(vec.reciprocal(rstd[:, q], std[:, q]))
                if ln == 2 and part == 0:
                    dve.wait_ge(s_tab, 32)
                for i in tiles:
                    last = vec.tensor_scalar(xn[:, i, :], x[:, i, :], meanvar[:, i, 0:1], rstd[:, i:i + 1],
                                             ALU.subtract, ALU.mult)
                    if i % 4 == 3:
                        last.then_inc(s_xn, 1)

            def choose(n):
                for r in range(2):
                    tiles = range(TILES // 2 * r, TILES // 2 * (r + 1))
                    q = slice(tiles[0], tiles[-1] + 1)
                    dve.wait_ge(s_sc, 2 * n + r + 1)
                    sc4 = scores[:, q, :].rearrange("p i (g e) -> p i g e", g=NG)
                    step(vec.tensor_reduce(gmax[:, q, 0:NG], sc4, AX, ALU.max))
                    for i in tiles:
                        last = vec.max(gtop[:, i, :], gmax[:, i, 0:NG])
                    step(last)
                    step(vec.memset(gtop[:, q, TOPG:8], -1.0))
                    for i in tiles:
                        last = vec.match_replace(gleft[:, i, :], gtop[:, i, :], gmax[:, i, :], 2.0)
                    step(last)
                    step(vec.tensor_scalar(gsel[:, q, :], gleft[:, q, 0:NG], 1.5, None, ALU.is_gt))
                    step(vec.tensor_tensor(sc4, sc4, gsel[:, q, :].unsqueeze(3).to_broadcast([P, len(tiles), NG, EG]),
                                           ALU.mult))
                    if r == 1:
                        for k in range(2):
                            dve.wait_ge(s_ssilu, 2 * n + k + 1)
                            vec.tensor_tensor(hs[:, k, :], hs[:, k, :], bank[2 + k][:, :], ALU.mult).then_inc(s_sh, 1)
                    for i in tiles:
                        last = vec.max(top[:, i, :], scores[:, i, :])
                    step(last)
                    for i in tiles:
                        last = vec.match_replace(left[:, i, :], top[:, i, :], scores[:, i, :], -1.0)
                    step(last)
                    vec.tensor_scalar(sel[:, :, q].rearrange("p e i -> p i e"), left[:, q, :], 0.0, None, ALU.is_lt)\
                        .then_inc(s_sel, 1)
                step(vec.tensor_reduce(wsum[:, :], top[:, :, :], AX, ALU.add))
                step(vec.tensor_scalar(wsum[:, :], wsum[:, :], 1e-9, None, ALU.max))
                step(vec.reciprocal(wsum[:, :], wsum[:, :]))
                step(vec.tensor_scalar(wsum[:, :], wsum[:, :], 1.25, None, ALU.mult))
                if n == 1:
                    dve.wait_ge(s_tab, 32)
                step(vec.scalar_tensor_tensor(out=wdense[:, :, :], in0=left[:, :, :], scalar=0.0,
                                              in1=scores[:, :, :], op0=ALU.is_lt, op1=ALU.mult))
                vec.tensor_tensor(wdense[:, :, :], wdense[:, :, :], wsum[:, :].unsqueeze(2).to_broadcast([P, TILES, E]),
                                  ALU.mult).then_inc(s_wdn, 1)

            def slots(n):
                dve.wait_ge(s_bas, n + 1)
                vec.tensor_copy(base[:, :], bank[6][:, 0:CH])
                vec.tensor_copy(ext[:, :, 0], bank[6][:, 0:CH])
                step(vec.tensor_tensor(end[:, :], bank[6][:, 0:CH], incl[:, :, P - 1], ALU.add))
                io = iota[:, 0:CAP].unsqueeze(1).to_broadcast([P, CH, CAP])
                vec.tensor_tensor(is_from[:, :, :], io, base[:, :].unsqueeze(2).to_broadcast([P, CH, CAP]), ALU.is_ge)
                step(vec.tensor_tensor(is_to[:, :, :], io, end[:, :].unsqueeze(2).to_broadcast([P, CH, CAP]), ALU.is_lt))
                step(vec.tensor_tensor(is_from[:, :, :], is_from[:, :, :], is_to[:, :, :], ALU.mult))
                def one_hot_tiles(c):
                    vec.tensor_tensor(slot_tile[:, c, :, :],
                                      is_from[:, c, :].unsqueeze(1).to_broadcast([P, EC, CAP]),
                                      own[:, :].unsqueeze(2).to_broadcast([P, EC, CAP]), ALU.mult).then_inc(s_slt, 1)

                one_hot_tiles(0)
                one_hot_tiles(1)
                for c in range(CH + 1):
                    if c < CH:
                        q = slice(4 * c, 4 * c + 4)
                        got = bank[6 + c % 2][:, 64 + 12 * c:76 + 12 * c].rearrange("p (j k) -> p j k", k=3)
                        dve.wait_ge(s_pck, CH * n + c + 1)
                        vec.scalar_tensor_tensor(out=room[:, q], in0=got[:, :, 0], scalar=-1.0,
                                                 in1=slot_half.to_broadcast([P, 4]), op0=ALU.mult, op1=ALU.add)\
                            .then_inc(s_room, 1)
                        vec.tensor_copy(picked[:, q, :], got).then_inc(s_picked, 1)
                        if c + 2 < CH:
                            one_hot_tiles(c + 2)
                    if c > 0:
                        q = slice(4 * c - 4, 4 * c)
                        dve.wait_ge(s_cmp, CH * n + c)
                        dve.wait_ge(s_picked, CH * n + c)
                        step(vec.scalar_tensor_tensor(out=token[:, q], in0=count[:, q], scalar=0.5, in1=picked[:, q, 1],
                                                      op0=ALU.mult, op1=ALU.add))
                        vec.tensor_copy(token_u[:, q], token[:, q]).then_inc(s_tok, 1)
                        if c % 2 == 0:
                            shared_add(n, c // 2 - 1)

            def shared_add(n, g):
                dve.wait_ge(s_sdn, 4 * n + g + 1)
                vec.scalar_tensor_tensor(
                    out=x[:, 4 * g:4 * g + 4, :], in0=bank[SHARED_BANK[g]][:, :].rearrange("p (i c) -> p i c", c=C), scalar=0.5,
                    in1=x[:, 4 * g:4 * g + 4, :], op0=ALU.mult, op1=ALU.add).then_inc(s_sx, 1)

            def build(n, tile):
                u = tile % 2 if isinstance(tile, int) else tile[1]
                rel = token_rel[:, tile:tile + 1, :] if isinstance(tile, int) \
                    else token_rel[:, bass.ds(tile[0] * 2 + (u + 2), 1), :]
                vec.tensor_tensor(onehot[:, u, :, :], iota_b[:, :].unsqueeze(1).to_broadcast([P, PAIRS, P]),
                                  rel.rearrange("p a j -> p (a j)").unsqueeze(2).to_broadcast([P, PAIRS, P]),
                                  ALU.is_equal).then_inc(s_oh[n], 1)

            def weight_outputs(n, k):
                dve.wait_ge(s_dn, CH * n + k + 1)
                dve.wait_ge(s_wsl, CH * n + k + 1)
                if k >= 2:
                    dve.wait_ge(s_left, CH * n + k - 1)
                vec.tensor_tensor(y_all[:, k % 2, :].rearrange("p (j c) -> p j c", c=C),
                                  bank[6 + k % 2][:, :].rearrange("p (j c) -> p j c", c=C),
                                  wslot[:, 4 * k:4 * k + 4].unsqueeze(2).to_broadcast([P, 4, C]),
                                  ALU.mult).then_inc(s_yall, 1)

            def experts(n):
                for c in range(CH + 3):
                    if c < CH:
                        dve.wait_ge(s_ga[c], 64 * (n + 1))
                        for e2 in range(2):
                            q = slice(e2 * CAP, (e2 + 1) * CAP)
                            o = C + e2 + 4 * c * (ROW + 2)
                            w = bufB[q, o:o + 3 * (ROW + 2) + 1:ROW + 2]
                            last = vec.tensor_tensor(wslot[q, 4 * c:4 * c + 4], w, picked[q, 4 * c:4 * c + 4, 2], ALU.mult)
                        last.then_inc(s_wsl, 1)
                        dve.wait_ge(s_silu, CH * n + c + 1)
                        if c >= 2:
                            dve.wait_ge(s_htp, CH * n + c - 1)
                        for e2 in range(2):
                            q = slice(e2 * CAP, (e2 + 1) * CAP)
                            last = vec.tensor_tensor(hidden[q, c % 2, :, e2 * I:(e2 + 1) * I],
                                                     hg[q, c % 2, :].rearrange("p (j i) -> p j i", i=I),
                                                     bank[2 + c % 2][q, :].rearrange("p (j i) -> p j i", i=2 * I)[:, :, I:],
                                                     ALU.mult)
                        last.then_inc(s_h, 1)
                    if 1 <= c < CH:
                        weight_outputs(n, c - 1)
                    if 2 <= c < CH + 2:
                        k = c - 2
                        dve.wait_ge(s_hi, CH * n + k + 1)
                        if k >= 2:
                            dve.wait_ge(s_yw, CH * n + k - 1)
                        vec.tensor_tensor(y_left[:, k % 2, :], y_all[:, k % 2, :],
                                          yw[:, 4 * k:4 * k + 4, 0, :], ALU.subtract).then_inc(s_left, 1)
                    if c >= 3:
                        k = c - 3
                        dve.wait_ge(s_mid, CH * n + k + 1)
                        vec.tensor_tensor(yw[:, 4 * k:4 * k + 4, 2, :], y_left[:, k % 2, :],
                                          yw[:, 4 * k:4 * k + 4, 1, :], ALU.subtract).then_inc(s_yw, 1)
                    if c == CH // 2 - 1:
                        vec.tensor_reduce(far[:, :], picked[:, :, 1], AX, ALU.max).then_inc(s_fart, 1)
                        dve.wait_ge(s_tok, CH * (n + 1))
                        vec.scalar_tensor_tensor(out=token_rel[:, 0:TILES, :], in0=iota[:, 0:TILES].unsqueeze(2).to_broadcast([P, TILES, PAIRS]),
                                                 scalar=-float(P), in1=token[:, :].unsqueeze(1).to_broadcast([P, TILES, PAIRS]),
                                                 op0=ALU.mult, op1=ALU.add).then_inc(s_trel, 1)
                    if CH // 2 <= c < CH:
                        k = c - CH // 2
                        if k == 0:
                            dve.wait_ge(s_trel, n + 1)
                        last = vec.tensor_tensor(onehot[:, 0, 8 * k:8 * k + 8, :],
                                                 iota_b[:, :].unsqueeze(1).to_broadcast([P, 8, P]),
                                                 token_rel[:, 0, 8 * k:8 * k + 8].unsqueeze(2).to_broadcast([P, 8, P]),
                                                 ALU.is_equal)
                        if c == CH - 1:
                            last.then_inc(s_oh[n], 1)
                    if c == CH - 1:
                        dve.wait_ge(s_far, n + 1)
                        step(vec.tensor_reduce(far1[:, :], bank[0][0:1, 0:P], AX, ALU.max))
                        vec.tensor_copy(far_i[:, :], far1[:, :]).then_inc(s_far_i, 1)

                    if c == CH:
                        weight_outputs(n, c - 1)

            def combine(n):
                dve.sem_inc(s_sum[n], 2)
                dve.sem_inc(s_add[n], 2)
                build(n, 1)
                dve.wait_ge(s_far_i, n + 1)
                last_tile = dve.value_load(far_i[0:1, 0:1], min_val=0, max_val=TILES * P)
                with dve.Fori(0, TILES // 2) as it:
                    with dve.If(it * (2 * P) <= last_tile):
                        for u in range(2):
                            dve.wait_ge(s_cmb[n], it * 2 + (u + 1))
                            dve.wait_ge(s_add[n], it * 2 + (u + 1))
                            vec.tensor_reduce(y_sum[:, u, :], bank[u][:, 0:3 * C].rearrange("p (k c) -> p c k", k=3),
                                              AX, ALU.add).then_inc(s_sum[n], 1)
                            with dve.If(it * (2 * P) + 2 * P <= last_tile):
                                build(n, (it, u))
                            dve.wait_ge(s_sum[n], it * 2 + (u + 3))
                            xs = x[:, bass.ds(it * 2 + u, 1), :]
                            vec.tensor_tensor(xs, xs, y_sum[:, u:u + 1, :], ALU.add).then_inc(s_add[n], 1)
                step(vec.memset(far1[:, :], 0.0))
                vec.memset(far1[:, :], 0.0).then_inc(s_done, 1)

            def cast_constants():
                dve.wait_ge(s_const, 16)
                vec.tensor_copy(tri[:, :], tri_f).then_inc(s_cast, 1)
                vec.tensor_copy(before[:, :], before_f).then_inc(s_cast, 1)
                vec.tensor_copy(own[:, :], own_f).then_inc(s_cast, 1)
                vec.tensor_copy(iota_b[:, :], iota)
                vec.memset(hidden[:, :, :, :], 0.0)
                vec.tensor_copy(ext[:, :, 1], tile_start.to_broadcast([P, CH]))
                vec.tensor_copy(ext[:, :, 2], ones_col.to_broadcast([P, CH]))
                step(vec.memset(gmax[:, :, NG:], -1.0))

            def ffn(n):
                statistics(2 * n, n)
                normalise_tokens(2 * n, n)
                if n == 0:
                    cast_constants()
                choose(n)
                slots(n)
                experts(n)
                combine(n)

            def attention():
                statistics(1, 0)
                normalise_tokens(1, 0)
                statistics(1, 1)
                for part in (2, 3):
                    statistics(1, part)
                    normalise_tokens(1, part - 1)
                normalise_tokens(1, 3)

                def rotate_queries(b, g, parts):
                    wait(dve, s_qc, b * G + (g + 1))
                    for part in parts:
                        e2 = part % 2
                        q = slice(e2 * D, (e2 + 1) * D)
                        out = heads(g, e2)[0:D] if part < 2 else heads(g, e2)[D:P]
                        vec.tensor_tensor(out, q_raw[q, :, :],
                                          (cos_q if part < 2 else sin_q)[q].unsqueeze(1).to_broadcast([D, 2, T]),
                                          ALU.mult).then_inc(s_qrot, 1)

                def normalise(b, k, scores_next=None):
                    r = k % 4
                    wait(dve, s_exp, b * H + (k + 1))
                    vec.reciprocal(rinv[:, r, :], rsum[:, r, :]).then_inc(s_rinv, 1)
                    dve.wait_ge(s_rinv, b * H + (k + 1))
                    vec.tensor_scalar(pr[:, r, 0:P], pr[:, r, 0:P], rinv[:, r, 0:1], None, ALU.mult)
                    if scores_next is not None:
                        dve.wait_ge(s_qk, scores_next)
                    vec.tensor_scalar(pr[:, r, P:3 * P], pr[:, r, P:3 * P], rinv[:, r, 1:2], None, ALU.mult)\
                        .then_inc(s_nrm, 1)

                def row_max(b, h):
                    k = h % 2
                    vec.tensor_tensor_reduce(out=sm[:, k, 0:P], in0=bank[k][:, 0:P], in1=causal[:, P:2 * P],
                                             scale=-0.125, scalar=3e38, op0=ALU.add, op1=ALU.min,
                                             accum_out=nmax[:, k, 0:1])
                    vec.tensor_tensor_reduce(out=sm[:, k, P:3 * P], in0=bank[k][:, P:3 * P], in1=causal,
                                             scale=-0.125, scalar=3e38, op0=ALU.add, op1=ALU.min,
                                             accum_out=nmax[:, k, 1:2]).then_inc(s_max, 1)

                def add_o(b):
                    wait(dve, s_o, (b + 1) * HB)
                    xs = x[:, b * TPB:(b + 1) * TPB, :] if isinstance(b, int) else x[:, bass.ds(b * TPB, TPB), :]
                    vec.tensor_tensor(xs, xs, bank[7][:, 0:TPB * C].rearrange("p (j c) -> p j c", c=C), ALU.add)\
                        .then_inc(s_oadd, 1)

                def early_statistics(h):
                    tiles = LN_TILES[2][0]
                    if h == 0:
                        dve.wait_ge(s_oadd, B - 2)
                    if h < 6:
                        for i in (2 * h, 2 * h + 1):
                            last = vec.bn_stats(stats[:, i, :], x[:, i, :])
                        last.then_inc(s_early, 1)
                    elif h < 8:
                        dve.wait_ge(s_early, 6)
                        for i in range(6 * h - 36, 6 * h - 30):
                            last = vec.bn_aggr(meanvar[:, i, :], stats[:, i, :])
                        last.then_inc(s_early, 1)
                    else:
                        dve.wait_ge(s_early, 8)
                        variance(tiles)

                def sequence(b, first=False, last=False, tail=False):
                    for h in range(2 if tail else H):
                        if h >= 2 or not first:
                            normalise(b, h - 2, None if tail else b * H + (h + 1))
                        elif not tail:
                            dve.wait_ge(s_qk, b * H + (h + 1))
                        if not tail:
                            row_max(b, h)
                            if h in ROPE_AT:
                                rotate_queries(b, *ROPE_AT[h])
                            if h == 5:
                                wait(dve, s_pv, b * HB)
                                dve.wait_ge(s_kvn, b * TPB + TPB)
                                vec.tensor_copy(v, kvn[:, :, G * D:2 * G * D]).then_inc(s_v, 1)
                            if not first and h == 8:
                                add_o(b - 1)
                            if last and h < 9:
                                early_statistics(h)
                            if not last and h in ROPE0_AT:
                                rotate_queries(b + 1, 0, ROPE0_AT[h])
                    if tail:
                        normalise_tokens(2, 0)
                        add_o(B - 1)

                rotate_queries(0, 0, (0, 1, 2))
                sequence(0, first=True)
                with dve.Fori(1, B - 1) as b:
                    sequence(b)
                sequence(B - 1, last=True)
                sequence(B, tail=True)

            ffn(0)
            dve.wait_ge(s_done, 1)
            attention()
            dve.wait_ge(s_oadd, B)
            ffn(1)


def shape_constants(np):
    P, T, TILES, EC = 128, 256, 16, 8
    p = np.arange(P)[:, None]
    q = np.arange(P)[None, :]
    inv_freq = (1.0 / np.float32(10000.0) ** (np.arange(0, 64, 2, dtype=np.float32) / np.float32(64))).astype(np.float32)
    angle = (np.arange(T, dtype=np.float32)[:, None] * inv_freq[None, :]).astype(np.float32)
    cos, sin = np.cos(angle), np.sin(angle)
    ck = cos.reshape(2, P, 32).transpose(1, 0, 2).reshape(P, 64)
    sk = sin.reshape(2, P, 32).transpose(1, 0, 2).reshape(P, 64)
    parts = [
        p == q,
        p <= q,
        (p // TILES == q // TILES) & (p < q),
        p // TILES == np.arange(EC)[None, :],
        p % TILES * P + P // 2,
        np.ones((P, 1)),
        p % 64 + 0.5,
        np.zeros((P, 1)) + q,
        np.zeros((P, P)), np.where(q <= p, 0.0, -1e30),
        np.concatenate([cos] * 4, axis=1).T,
        np.concatenate([sin, -sin, sin, -sin], axis=1).T,
        ck, sk, -sk,
    ]
    return np.ascontiguousarray(np.concatenate([a.astype(np.float32) for a in parts], axis=1))


def kernel(**inputs):
    import numpy as np
    import concourse.bacc as bacc
    from concourse.bass_utils import run_bass_kernel_spmd

    a = {n[3:]: np.asarray(v) for n, v in inputs.items()}
    wq = a["attn_Wq"].reshape(128, 16, 32, 2)
    even, odd = wq[..., 0], wq[..., 1]
    wk = a["attn_Wk"].reshape(128, 4, 32, 2)
    arrays = {
        "x": a["attn_x"],
        "wq": np.concatenate([even, odd], axis=2),
        "wkv": np.concatenate([wk.transpose(0, 1, 3, 2).reshape(128, 256), a["attn_Wv"]], axis=1),
        "wo": a["attn_Wo"],
        "router": a["ffn_router_w"],
        "gate_up": np.concatenate([a["ffn_gate_w"], a["ffn_up_w"]], axis=2).transpose(1, 0, 2),
        "down": a["ffn_down_w"].reshape(32, 128, 128).transpose(1, 0, 2),
        "shared_gate": a["ffn_shared_gate_w"],
        "shared_up": a["ffn_shared_up_w"],
        "shared_down": a["ffn_shared_down_w"],
        "shape_constants": shape_constants(np),
    }
    arrays = {n: np.ascontiguousarray(v) for n, v in arrays.items()}
    nc = bacc.Bacc("TRN2", target_bir_lowering=False, num_devices=1)
    args = [nc.dram_tensor(f"{n}_dram", v.shape, mybir.dt.from_np(v.dtype), kind="ExternalInput").ap() for n, v in arrays.items()]
    args.append(nc.dram_tensor("result", (8, 256, 128), mybir.dt.float32, kind="ExternalOutput").ap())
    macaron_block(nc, *args)
    r = run_bass_kernel_spmd(nc, [{f"{n}_dram": v for n, v in arrays.items()}], core_ids=[0])
    return r.results[0]["result"]
```
